# Optimizing a Trainium2 kernel written in Bass

```python
import numpy as np
import jax
import jax.numpy as jnp

def _softmax(x, axis=-1):
    return jax.nn.softmax(x, axis=axis)

def _gelu(x):
    return jax.nn.gelu(x, approximate=True)

def _silu(x):
    return jax.nn.silu(x)

def _sigmoid(x):
    return jax.nn.sigmoid(x)

def _layernorm(x, axis=-1, eps=1e-05):
    m = jnp.mean(x, axis=axis, keepdims=True)
    v = jnp.var(x, axis=axis, keepdims=True)
    return (x - m) / jnp.sqrt(v + eps)

def _scatter_add(tgt, idx, src, axis=0):
    return tgt.at[idx].add(src)

def _segment_sum(src, seg, n):
    return jax.ops.segment_sum(src, seg, n)
kernel_name = 'mk_decoder_postln_d1_seqx_r8_aa621c'

def setup_inputs(seed: int=0):
    np.random.seed(seed)
    _w = jnp.asarray

    def _rec_inputs():
        import jax
        import jax.numpy as jnp
        _rk = jax.random.key(seed)
        x = 7.22e-05 + 1 * jax.random.normal(jax.random.fold_in(_rk, 1), (64, 64, 256), jnp.float32)
        _lenS = 64 - jax.random.randint(jax.random.fold_in(_rk, 7), (64,), 0, max(1, 64 // 4) + 1, jnp.int32)
        _lenS2 = 64 - jax.random.randint(jax.random.fold_in(_rk, 8), (64,), 0, max(1, 64 // 4) + 1, jnp.int32)
        _ctx_1024P = jax.random.normal(jax.random.fold_in(_rk, 11), (64, 16, 128), jnp.float32)
        _ctx_1024c = jax.random.dirichlet(jax.random.fold_in(_rk, 511), 0.3 * jnp.ones((16,), jnp.float32), (64, 64))
        _ctx_1024t = jnp.einsum('bsk,bkd->bsd', _ctx_1024c, _ctx_1024P)
        _ctx_1024t = _ctx_1024t * jax.lax.rsqrt(jnp.mean(jnp.square(_ctx_1024t)) + 1e-12) * 0.953939
        ctx_1024 = -1.39393e-06 + 0.999914 * (_ctx_1024t + 0.3 * jax.random.normal(jax.random.fold_in(_rk, 611), (64, 64, 128), jnp.float32))
        fside_BxSx2_0 = jax.random.uniform(jax.random.fold_in(_rk, 12), (64, 64, 2), jnp.float32, 0.0, 0.999707)
        return (x, ctx_1024, fside_BxSx2_0)
    x, ctx_1024, fside_BxSx2_0 = _rec_inputs()

    def _L0_attn_setup():
        import jax, jax.numpy as jnp
        import numpy as np
        import math
        E = 256
        H = 16
        D = E // H

        def _alibi_slopes(n):

            def pow2_slopes(n):
                start = 2 ** (-2 ** (-(math.log2(n) - 3)))
                return [start * start ** i for i in range(n)]
            if math.log2(n).is_integer():
                return pow2_slopes(n)
            c = 2 ** math.floor(math.log2(n))
            return pow2_slopes(c) + _alibi_slopes(2 * c)[::2][:n - c]

        def _alibi_bias(seq_len):
            slopes = jnp.asarray(_alibi_slopes(H), dtype=jnp.float32)
            pos = jnp.arange(seq_len)
            rel = jnp.abs(pos[None, :] - pos[:, None]).astype(jnp.float32)
            return -slopes[:, None, None] * rel[None, :, :]
        key = jax.random.key(seed)
        ks = jax.random.split(key, 5)
        B, S = (2, 256)
        scale = 1.0 / math.sqrt(E)
        x = jax.random.normal(ks[0], (B, S, E), dtype=jnp.float32)
        Wq = jax.random.normal(ks[1], (E, E), dtype=jnp.float32) * scale
        Wk = jax.random.normal(ks[2], (E, E), dtype=jnp.float32) * scale
        Wv = jax.random.normal(ks[3], (E, E), dtype=jnp.float32) * scale
        Wo = jax.random.normal(ks[4], (E, E), dtype=jnp.float32) * scale
        z = jnp.zeros((E,), dtype=jnp.float32)
        return {'x': x, 'Wq': Wq, 'bq': z, 'Wk': Wk, 'bk': z, 'Wv': Wv, 'bv': z, 'Wo': Wo, 'bo': z}
    _L0_attn_all = _L0_attn_setup()
    _L0_attn_in = {k: v for k, v in _L0_attn_all.items() if k in ('Wq', 'bq', 'Wk', 'bk', 'Wv', 'bv', 'Wo', 'bo')}
    del _L0_attn_all

    def _L0_xattn_setup():
        import jax, jax.numpy as jnp
        import numpy as np
        DIM = 256
        CTX_DIM = 128
        N_HEADS = 32
        HEAD_DIM = DIM // N_HEADS
        POS_DIM = 2
        B, N, CTXN = (2, 256, 256)
        ROPE_BASE = 10000.0

        def apply_axial_rope(x, pos):
            b, n, h, d = x.shape
            p = pos.shape[-1]
            dpa = d // p
            half = dpa // 2
            freqs = ROPE_BASE ** (-jnp.arange(half, dtype=x.dtype) / half)
            ang = pos[..., :, None] * freqs
            cos = jnp.cos(ang)[:, :, None, :, :]
            sin = jnp.sin(ang)[:, :, None, :, :]
            xr = x.reshape(b, n, h, p, half, 2)
            x1, x2 = (xr[..., 0], xr[..., 1])
            out = jnp.stack([x1 * cos - x2 * sin, x1 * sin + x2 * cos], axis=-1)
            return out.reshape(b, n, h, d)
        key = jax.random.key(seed)
        ks = jax.random.split(key, 8)
        x = jax.random.normal(ks[0], (B, N, DIM), jnp.float32)
        ctx = jax.random.normal(ks[1], (B, CTXN, CTX_DIM), jnp.float32)
        pos_map = jax.random.uniform(ks[2], (B, N, POS_DIM), jnp.float32)
        ctx_pos_map = jax.random.uniform(ks[3], (B, CTXN, POS_DIM), jnp.float32)
        Wq = jax.random.normal(ks[4], (DIM, DIM), jnp.float32) / np.sqrt(DIM)
        Wkv = jax.random.normal(ks[5], (CTX_DIM, 2 * DIM), jnp.float32) / np.sqrt(CTX_DIM)
        Wout = jax.random.normal(ks[6], (DIM, DIM), jnp.float32) / np.sqrt(DIM)
        bout = jnp.zeros((DIM,), jnp.float32)
        return {'x': x, 'ctx': ctx, 'pos_map': pos_map, 'ctx_pos_map': ctx_pos_map, 'Wq': Wq, 'Wkv': Wkv, 'Wout': Wout, 'bout': bout}
    _L0_xattn_all = _L0_xattn_setup()
    _L0_xattn_in = {k: v for k, v in _L0_xattn_all.items() if k in ('Wq', 'Wkv', 'Wout', 'bout')}
    del _L0_xattn_all

    def _L0_ffn_setup():
        import jax, jax.numpy as jnp
        import numpy as np
        DIM_IN = 256
        DIM_HIDDEN = 1024
        key = jax.random.key(seed)
        k_x, k_g, k_u, k_d = jax.random.split(key, 4)
        s_in = 1.0 / np.sqrt(DIM_IN)
        s_hid = 1.0 / np.sqrt(DIM_HIDDEN)
        x = jax.random.normal(k_x, (4, 256, DIM_IN), dtype=jnp.float32)
        w_gate = jax.random.uniform(k_g, (DIM_HIDDEN, DIM_IN), jnp.float32, -s_in, s_in)
        w_up = jax.random.uniform(k_u, (DIM_HIDDEN, DIM_IN), jnp.float32, -s_in, s_in)
        w_down = jax.random.uniform(k_d, (DIM_IN, DIM_HIDDEN), jnp.float32, -s_hid, s_hid)
        return {'x': x, 'w_gate': w_gate, 'w_up': w_up, 'w_down': w_down}
    _L0_ffn_all = _L0_ffn_setup()
    _L0_ffn_in = {k: v for k, v in _L0_ffn_all.items() if k in ('w_gate', 'w_up', 'w_down')}
    del _L0_ffn_all
    return {'x': x, 'ctx_1024': ctx_1024, 'fside_BxSx2_0': fside_BxSx2_0, 'L0_attn_Wq': _L0_attn_in['Wq'], 'L0_attn_bq': _L0_attn_in['bq'], 'L0_attn_Wk': _L0_attn_in['Wk'], 'L0_attn_bk': _L0_attn_in['bk'], 'L0_attn_Wv': _L0_attn_in['Wv'], 'L0_attn_bv': _L0_attn_in['bv'], 'L0_attn_Wo': _L0_attn_in['Wo'], 'L0_attn_bo': _L0_attn_in['bo'], 'L0_xattn_Wq': _L0_xattn_in['Wq'], 'L0_xattn_Wkv': _L0_xattn_in['Wkv'], 'L0_xattn_Wout': _L0_xattn_in['Wout'], 'L0_xattn_bout': _L0_xattn_in['bout'], 'L0_ffn_w_gate': _L0_ffn_in['w_gate'], 'L0_ffn_w_up': _L0_ffn_in['w_up'], 'L0_ffn_w_down': _L0_ffn_in['w_down']}

def reference(x, ctx_1024, fside_BxSx2_0, L0_attn_Wq, L0_attn_bq, L0_attn_Wk, L0_attn_bk, L0_attn_Wv, L0_attn_bv, L0_attn_Wo, L0_attn_bo, L0_xattn_Wq, L0_xattn_Wkv, L0_xattn_Wout, L0_xattn_bout, L0_ffn_w_gate, L0_ffn_w_up, L0_ffn_w_down):
    import jax
    import jax.numpy as jnp

    def _L0_attn_ref(x, Wq, bq, Wk, bk, Wv, bv, Wo, bo):
        import jax, jax.numpy as jnp
        import numpy as np
        import math
        E = 256
        H = 16
        D = E // H

        def _alibi_slopes(n):

            def pow2_slopes(n):
                start = 2 ** (-2 ** (-(math.log2(n) - 3)))
                return [start * start ** i for i in range(n)]
            if math.log2(n).is_integer():
                return pow2_slopes(n)
            c = 2 ** math.floor(math.log2(n))
            return pow2_slopes(c) + _alibi_slopes(2 * c)[::2][:n - c]

        def _alibi_bias(seq_len):
            slopes = jnp.asarray(_alibi_slopes(H), dtype=jnp.float32)
            pos = jnp.arange(seq_len)
            rel = jnp.abs(pos[None, :] - pos[:, None]).astype(jnp.float32)
            return -slopes[:, None, None] * rel[None, :, :]
        B, S, _ = x.shape

        def proj(W, b):
            return (x @ W.T + b).reshape(B, S, H, D).transpose(0, 2, 1, 3)
        q = proj(Wq, bq)
        k = proj(Wk, bk)
        v = proj(Wv, bv)
        scores = jnp.einsum('bhqd,bhkd->bhqk', q, k) / math.sqrt(D)
        causal = jnp.triu(jnp.ones((S, S), dtype=bool), k=1)
        scores = jnp.where(causal[None, None], -jnp.inf, scores)
        scores = scores + _alibi_bias(S)[None]
        probs = jax.nn.softmax(scores, axis=-1)
        out = jnp.einsum('bhqk,bhkd->bhqd', probs, v)
        out = out.transpose(0, 2, 1, 3).reshape(B, S, E)
        return out @ Wo.T + bo

    def _L0_xattn_ref(x, ctx, pos_map, ctx_pos_map, Wq, Wkv, Wout, bout):
        import jax, jax.numpy as jnp
        import numpy as np
        DIM = 256
        CTX_DIM = 128
        N_HEADS = 32
        HEAD_DIM = DIM // N_HEADS
        POS_DIM = 2
        B, N, CTXN = (2, 256, 256)
        ROPE_BASE = 10000.0

        def apply_axial_rope(x, pos):
            b, n, h, d = x.shape
            p = pos.shape[-1]
            dpa = d // p
            half = dpa // 2
            freqs = ROPE_BASE ** (-jnp.arange(half, dtype=x.dtype) / half)
            ang = pos[..., :, None] * freqs
            cos = jnp.cos(ang)[:, :, None, :, :]
            sin = jnp.sin(ang)[:, :, None, :, :]
            xr = x.reshape(b, n, h, p, half, 2)
            x1, x2 = (xr[..., 0], xr[..., 1])
            out = jnp.stack([x1 * cos - x2 * sin, x1 * sin + x2 * cos], axis=-1)
            return out.reshape(b, n, h, d)
        b, n, _ = x.shape
        ctx_n = ctx.shape[1]
        q = (x @ Wq).reshape(b, n, N_HEADS, HEAD_DIM)
        k, v = jnp.split(ctx @ Wkv, 2, axis=-1)
        k = k.reshape(b, ctx_n, N_HEADS, HEAD_DIM)
        v = v.reshape(b, ctx_n, N_HEADS, HEAD_DIM)
        q = apply_axial_rope(q, pos_map)
        k = apply_axial_rope(k, ctx_pos_map)
        scale = 1.0 / np.sqrt(HEAD_DIM).astype(np.float32)
        logits = jnp.einsum('bqhd,bkhd->bhqk', q, k) * scale
        w = jax.nn.softmax(logits, axis=-1)
        attn = jnp.einsum('bhqk,bkhd->bqhd', w, v)
        attn = attn.reshape(b, n, N_HEADS * HEAD_DIM)
        return attn @ Wout + bout

    def _L0_ffn_ref(x, w_gate, w_up, w_down):
        import jax, jax.numpy as jnp
        import numpy as np
        DIM_IN = 256
        DIM_HIDDEN = 1024
        gate = jnp.einsum('bsd,hd->bsh', x, w_gate)
        up = jnp.einsum('bsd,hd->bsh', x, w_up)
        gated = jax.nn.silu(gate) * up
        return jnp.einsum('bsh,dh->bsd', gated, w_down)
    x = _layernorm(x + _L0_attn_ref(x, L0_attn_Wq, L0_attn_bq, L0_attn_Wk, L0_attn_bk, L0_attn_Wv, L0_attn_bv, L0_attn_Wo, L0_attn_bo), axis=-1)
    x = _layernorm(x + _L0_xattn_ref(x, ctx_1024, fside_BxSx2_0, fside_BxSx2_0, L0_xattn_Wq, L0_xattn_Wkv, L0_xattn_Wout, L0_xattn_bout), axis=-1)
    x = _layernorm(x + _L0_ffn_ref(x, L0_ffn_w_gate, L0_ffn_w_up, L0_ffn_w_down), axis=-1)
    return x

_drawn_inputs = setup_inputs


def setup_inputs(seed=0):
    import zlib

    import numpy as np

    out = dict(_drawn_inputs(seed))
    spreads = {'L0_attn_bq': (0.0, 0.334),
     'L0_attn_bk': (0.0, 0.8),
     'L0_attn_bv': (0.0, 0.1),
     'L0_attn_bo': (0.0, 0.1),
     'L0_xattn_bout': (0.0, 0.1)}
    factors = {}
    for name, (base, spread) in spreads.items():
        noise = np.random.default_rng([zlib.crc32(name.encode()), seed]).standard_normal(out[name].shape)
        drawn = base * np.exp(spread * noise) if base else spread * noise
        out[name] = jnp.asarray(drawn.astype(out[name].dtype))
    for name, factor in factors.items():
        out[name] = (out[name] * factor).astype(out[name].dtype)
    return out
```

```python
from contextlib import ExitStack

import concourse.bass as bass
from concourse import mybir

F32 = mybir.dt.float32
F32R = mybir.dt.float32r
F16 = mybir.dt.float16
BF16 = mybir.dt.bfloat16
ALU = mybir.AluOpType
ACT = mybir.ActivationFunctionType
AX_X = mybir.AxisListType.X

P = 128
SEQ = 64
NSEQ = 64
E = 256
CTX = 128
HID = 1024
TOK = 256
NT = NSEQ * SEQ // TOK
BPT = TOK // SEQ
NG = 8
EC = E // P
VW = 64
LN_EPS = 1e-5
M_CLAMP = 60000.0
SELF_CONST = 6
TWO_PI = (6.28125, 0.0019350051879882812, 3.0199159819149963e-07)
INV_TWO_PI = 0.15915494309189535
ROUND = 12582912.0
PI_IN = 3.1415925
HALF_PI = 1.5707963267948966


class Tile:

    def __init__(self, turn, parity):
        self.turn, self.parity = turn, parity
        self.n = turn * 2 + parity

    def back(self, k):
        m = self.parity - k
        return Tile(self.turn + m // 2 if m >= 0 else self.turn - (-m + 1) // 2, m % 2)


def there(t, tiles=NT):
    return not isinstance(t.n, int) or 0 <= t.n < tiles


def nth(t, per_tile, k):
    return t.n * per_tile + k


def dmas(t, count):
    return (t.turn + 1) * (16 * count)


def waits_alone(eng):
    eng.nop(nofuse=True)


def run_slots(eng, slot, first, last, tiles=NT):
    for s in range(first):
        slot(Tile(s // 2, s % 2))
    with eng.Fori(first // 2, tiles // 2) as turn:
        for parity in range(2):
            slot(Tile(turn, parity))
    for s in range(tiles, last + 1):
        slot(Tile(s // 2, s % 2))


def mm3(nc, out, w_hi, w_lo, x_hi, x_lo, first, last):
    nc.tensor.matmul(out, w_hi, x_hi, start=first, stop=False)
    nc.tensor.matmul(out, w_hi, x_lo, start=False, stop=False)
    return nc.tensor.matmul(out, w_lo, x_hi, start=False, stop=last)


def split_weights(nc, parts):
    with nc.semaphore("w_loaded") as loaded, nc.semaphore("w_scaled") as scaled, \
            nc.semaphore("w_hi_done") as hi_done, nc.semaphore("w_lo_done") as lo_done, nc.Block() as block:
        @block.sync
        def _(sp):
            for dram, raw, _, _, _ in parts:
                sp.dma_start(raw, dram).then_inc(loaded, 16)

        @block.vector
        def _(dve):
            dve.wait_ge(loaded, 16 * len(parts))
            for n, (_, raw, hi, lo, scale) in enumerate(parts):
                nc.vector.tensor_scalar(raw, raw, scale, None, ALU.mult).then_inc(scaled, 1)
                dve.wait_ge(scaled, n + 1)
                nc.vector.tensor_copy(hi, raw).then_inc(hi_done, 1)
                dve.wait_ge(hi_done, n + 1)
                nc.vector.tensor_tensor(lo, raw, hi.bitcast(F32), ALU.subtract).then_inc(lo_done, 1)
            dve.wait_ge(lo_done, len(parts))


def rotary_tables(nc, pos_dram, cols_dram, cs_dram):
    n = NSEQ * SEQ
    with ExitStack() as ctx:
        def sb(name, shape, dt):
            return ctx.enter_context(nc.sbuf_tensor(f"r_{name}", shape, dt))

        pos = sb("pos", [P, n], F32)
        turns = sb("turns", [P, n], F32)
        cos_arg = sb("cos_arg", [P, n], F32)
        cols = sb("cols", [P, 2], F32)
        loaded = ctx.enter_context(nc.semaphore("r_loaded"))
        step = ctx.enter_context(nc.semaphore("r_step"))
        sined = ctx.enter_context(nc.semaphore("r_sined"))
        stored = ctx.enter_context(nc.semaphore("r_stored"))
        block = ctx.enter_context(nc.Block())

        @block.sync
        def _(sp):
            sp.dma_start(pos[:], pos_dram).then_inc(loaded, 16)
            sp.dma_start(cols[:], cols_dram).then_inc(loaded, 16)
            sp.wait_ge(sined, 2)
            sp.dma_start(cs_dram[0], cos_arg[:]).then_inc(stored, 16)
            sp.wait_ge(step, 10)
            sp.dma_start(cs_dram[1], pos[:]).then_inc(stored, 16)
            sp.wait_ge(stored, 32)

        @block.vector
        def _(dve):
            dve.wait_ge(loaded, 32)
            nc.vector.tensor_scalar(pos[:], pos[:], cols[:, 0:1], None, ALU.mult).then_inc(step, 1)
            dve.wait_ge(step, 1)
            nc.vector.tensor_scalar(turns[:], pos[:], INV_TWO_PI, ROUND, ALU.mult, ALU.add).then_inc(step, 1)
            dve.wait_ge(step, 2)
            nc.vector.tensor_scalar(turns[:], turns[:], ROUND, None, ALU.subtract).then_inc(step, 1)
            for k, part in enumerate(TWO_PI):
                dve.wait_ge(step, 3 + k)
                nc.vector.scalar_tensor_tensor(pos[:], turns[:], -part, pos[:], ALU.mult, ALU.add).then_inc(step, 1)
            dve.wait_ge(step, 6)
            nc.vector.tensor_scalar(pos[:], pos[:], PI_IN, -PI_IN, ALU.min, ALU.max).then_inc(step, 1)
            dve.wait_ge(step, 7)
            nc.vector.scalar_tensor_tensor(cos_arg[:], pos[:], -1.0, pos[:], ALU.mult, ALU.max).then_inc(step, 1)
            dve.wait_ge(step, 8)
            nc.vector.tensor_scalar(cos_arg[:], cos_arg[:], -1.0, HALF_PI, ALU.mult, ALU.add).then_inc(step, 1)
            dve.wait_ge(sined, 1)
            nc.vector.tensor_scalar(pos[:], pos[:], cols[:, 1:2], None, ALU.mult).then_inc(step, 1)

        @block.scalar
        def _(act):
            act.wait_ge(step, 9)
            nc.scalar.activation(pos[:], pos[:], ACT.Sin).then_inc(sined, 1)
            nc.scalar.activation(cos_arg[:], cos_arg[:], ACT.Sin).then_inc(sined, 1)


def attention(nc, heads, d_head, rope, src, kv_src, w_dram, x_out, consts):
    G = heads // NG
    SPLIT = 3 * d_head * G
    CONST = 0 if rope else SELF_CONST
    ROWS_M = SPLIT + CONST
    ROWS_X = ROWS_M + 1
    NX = heads * SEQ // 512
    MCOL = NG * BPT * G // 2
    POB = heads * VW // 2 // 512
    KC = 1 if rope else EC
    pre = "x" if rope else "s"

    with ExitStack() as ctx:
        def sb(name, shape, dt):
            return ctx.enter_context(nc.sbuf_tensor(f"{pre}_{name}", shape, dt))

        def ps(name, shape):
            return ctx.enter_context(nc.psum_tensor(f"{pre}_{name}", shape, F32))

        def sem(name):
            return ctx.enter_context(nc.semaphore(f"{pre}_{name}"))

        wq = [sb(f"wq{i}", [P, EC, E], F32R) for i in range(2)]
        wk = [sb(f"wk{i}", [P, KC, E], F32R) for i in range(2)]
        wv = [sb(f"wv{i}", [P, KC, E], F32R) for i in range(2)]
        wo = [sb(f"wo{i}", [P, EC, E], F32R) for i in range(2)]
        with ExitStack() as raw_ctx:
            raws = [raw_ctx.enter_context(nc.sbuf_tensor(f"{pre}_raw{i}", [P, k, E], F32))
                    for i, k in enumerate((EC, KC, KC, EC))]
            q_scale = 1.0 if rope else d_head ** -0.5
            split_weights(nc, [(w_dram[n], r[:], w[0][:], w[1][:], q_scale if n == "wq" else 1.0)
                               for n, r, w in zip(("wq", "wk", "wv", "wo"), raws, (wq, wk, wv, wo))])

        qin = None if rope else [sb(f"qin{i}", [P, EC, TOK], F32) for i in range(2)]
        kvin = [sb(f"kvin{i}", [P, KC, TOK], F32) for i in range(2)] if rope else None
        tok_in = [sb(f"tok{i}", [P, 2, E], F32) for i in range(2)]
        tok_a = [sb(f"toka{i}", [P, 2, E], F32) for i in range(2)] if rope else None
        kv_hi = [sb(f"kv_hi{i}", [P, KC, TOK], F32R) for i in range(2)]
        kv_lo = [sb(f"kv_lo{i}", [P, KC, TOK], F32R) for i in range(2)]
        q_hi = [sb("q_hi", [P, EC, TOK], F32R)] if rope else kv_hi
        q_lo = [sb("q_lo", [P, EC, TOK], F32R)] if rope else kv_lo
        qk16 = sb("qk16", [P, 2, 2, EC, TOK], F16)
        if rope:
            cs = [sb(f"cs{i}", [P, 2, TOK], F32) for i in range(2)]
            rot = sb("rot", [P, 2, 3, EC, TOK], F32)
        K3 = [sb(f"K3{i}", [ROWS_X, NG, TOK], F16) for i in range(2)]
        Qr = sb("Qr", [SPLIT, NG, TOK], F16)
        head_rows = sb("head_rows", [SPLIT, G], F32)
        Q3 = [sb(f"Q3{i}", [ROWS_X, NG, BPT, G * SEQ], F16) for i in range(2)]
        Vb = [sb(f"Vb{i}", [P, 2, heads, VW], F32) for i in range(2)]
        PT = [sb(f"PT{i}", [P, heads * SEQ], F32) for i in range(2)]
        mx = sb("mx", [P, MCOL], F32)
        mT = sb("mT", [MCOL, P], F16)
        rec = sb("rec", [P, 2, heads // 2, 2], F32)
        On = sb("On", [P, 2, 2, E // 2], F32)
        aT_hi, aT_lo = sb("aT_hi", [P, 2, 2, P], F32R), sb("aT_lo", [P, 2, 2, P], F32R)
        y = sb("y", [P, 2, E], F32)
        stats = sb("stats", [P, 2, 6], F32)
        mv = sb("mv", [P, 2, 2], F32)
        rstd = sb("rstd", [P, 2], F32)
        x_new = [sb(f"xn{i}", [P, 2, E], F32) for i in range(2)]
        bo_bc = sb("bo", [P, E], F32)
        minus_half = sb("mh", [P, 1], F32)
        ident = sb("ident", [P, P], F32)
        if not rope:
            ident_bf = sb("identb", [P, P], BF16)
            mask_q = sb("mask_q", [P, 512], BF16)
            mask_k = sb("mask_k", [P, 512], BF16)
            mask_raw = sb("mask_raw", [P, 2, 512], F32)
            bv_bc = sb("bv", [P, E], F32)
            bqk = sb("bqk", [P, 2, EC], F32)

        psX = [ps(f"psX{i}", [P, 512]) for i in range(2)]
        psM = [ps(f"psM{i}", [P, 512]) for i in range(2)]
        psJ = [ps(f"psJ{i}", [P, 512]) for i in range(2)]
        psO = ps("psO", [P, 2, 512])

        s_const = sem("const_loaded")
        s_in = [sem(f"in_loaded{i}") for i in range(2)]
        s_tok = [sem(f"tok_loaded{i}") for i in range(2)]
        s_init = sem("buffers_set")
        s_bq = sem("bq_scaled")
        s_mask = sem("masks_cast")
        s_split = sem("inputs_split")
        s_qkproj = sem("qk_projected")
        s_hi = sem("qk_high")
        s_lo = sem("qk_low")
        s_vproj = sem("v_projected")
        s_vb = sem("v_placed")
        s_scr = [sem(f"{n}_parts_stored") for n in "qk"]
        s_qr = sem("q_rows_loaded")
        s_k3 = [sem(f"k_rows_loaded{i}") for i in range(2)]
        s_q3 = sem("q_spread")
        s_mscore = sem("max_scores")
        s_mx = sem("maxima")
        s_mtr = sem("maxima_transposed")
        s_mt = sem("maxima_copied")
        s_mrow = [sem(f"shift_rows{i}") for i in range(2)]
        s_xscore = sem("scores")
        s_exp = sem("probs")
        s_pv = sem("pv_done")
        s_rec = sem("sums_inverted")
        s_on = sem("normalised")
        s_atr = sem("attn_transposed")
        s_ahi = sem("attn_high")
        s_alo = sem("attn_low")
        s_proj = sem("out_projected")
        s_xb = sem("residual_biased")
        s_y = sem("residual_added")
        s_stat = sem("stats_done")
        s_var = sem("variance_done")
        s_eps = sem("eps_added")
        s_rstd = sem("rstd_done")
        s_new = sem("normed")
        s_store = [sem(f"out_stored{i}") for i in range(2)]
        if rope:
            s_xtr = sem("input_transposed")
            s_xhi = sem("input_high")
            s_xlo = sem("input_low")
            s_plain = sem("rot_plain")
            s_swap = sem("rot_swapped")
            s_cos = sem("rot_by_cos")
            s_sin = sem("rot_by_sin")
            s_rot = sem("rotated")
        scratch = consts["scratch"]
        n_in = 3 if rope else 1
        hi_per = 2 if rope else 4
        STEPS = 2 * NX
        i_chunk = [slice(SEQ * b, SEQ * (b + 1)) for b in range(BPT)]

        const_loads = [(bo_bc[:], consts["bo"]), (ident[:], consts["ident"]), (head_rows[:], consts["head_rows"])]
        if not rope:
            const_loads += [(mask_raw[:, 0], consts["mask_q"]), (mask_raw[:, 1], consts["mask_k"]), (bv_bc[:], consts["bv"]), (bqk[:], consts["bqk"])]
        for i in range(2):
            const_loads += [(K3[i][SPLIT:ROWS_X, :, :], consts["k_rows"])]
            if not rope:
                const_loads += [(Q3[i][SPLIT:ROWS_M], consts["q_rows"])]
        def aT_ps():
            return psJ[0][:, 0:2 * P].rearrange("p (b r q) -> p b r q", b=2, r=2)

        def po(pr):
            banks = psO[:] if POB == 2 else psO[:, pr:pr + 1, :]
            return banks.rearrange("p b (h w) -> p (b h) w", w=VW)[:, :, 0:2 * (d_head + 1)].rearrange(
                "p h (b e) -> p h b e", e=d_head + 1)

        block = ctx.enter_context(nc.Block())

        @block.sync
        def _(sp):
            for dst, dram in const_loads:
                sp.dma_start(dst, dram).then_inc(s_const, 16)

            def slot(u):
                v, w, c, i = u.back(1), u.back(2), u.back(3), u.parity
                if there(u):
                    if there(w):
                        sp.wait_ge(s_split, nth(w, 2, 2))
                        if rope:
                            waits_alone(sp)
                            sp.wait_ge(s_xtr, nth(w, 1, 1))
                            sp.wait_ge(s_cos, nth(w, 2, 2))
                            sp.wait_ge(s_sin, nth(w, 2, 2))
                        waits_alone(sp)
                    if rope:
                        sp.dma_start(kvin[i][:], kv_src[:, :, bass.ds(u.n * TOK, TOK)]).then_inc(s_in[i], 16)
                        sp.dma_start(cs[i][:], consts["cs"][:, :, bass.ds(u.n * TOK, TOK)]).then_inc(s_in[i], 16)
                        sp.dma_start(tok_a[i][:], src["tok"][u.n]).then_inc(s_in[i], 16)
                    else:
                        sp.dma_start(qin[i][:], src["T"][:, :, bass.ds(u.n * TOK, TOK)]).then_inc(s_in[i], 16)
                if there(v):
                    i = v.parity
                    if there(v.back(2)):
                        sp.wait_ge(s_k3[i], dmas(v.back(2), 3))
                    for o in range(2):
                        sp.wait_ge(s_hi, nth(v, hi_per, hi_per // 2 * (o + 1)))
                        sp.wait_ge(s_lo, nth(v, hi_per, hi_per // 2 * (o + 1)))
                        sp.dma_start(scratch[i, o].rearrange("r g a n -> g r (a n)"),
                                     qk16[:, o].rearrange("p a c n -> p (a c n)")).then_inc(s_scr[o], 16)
                        sp.wait_ge(s_scr[o], (v.n + 1) * 16)
                        if there(v.back(2)):
                            if o:
                                sp.wait_ge(s_xscore, nth(v.back(2), STEPS, STEPS))
                            else:
                                sp.wait_ge(s_q3, nth(v.back(1), G, G))
                        for k, part in enumerate(((0, 1, 0), (0, 0, 1))[o]):
                            to = (Qr, K3[i])[o][bass.ts(k, E // NG)].rearrange("r g n -> r (g n)")
                            sp.dma_start(to, scratch[i, o, :, :, part]).then_inc((s_qr, s_k3[i])[o], 16)
                if there(w):
                    if there(w.back(2)):
                        sp.wait_ge(s_y, nth(w.back(2), 2, 2))
                        waits_alone(sp)
                    sp.dma_start(tok_in[w.parity][:], src["tok"][w.n]).then_inc(s_tok[w.parity], 16)
                if there(c):
                    sp.wait_ge(s_new, nth(c, 2, 2))
                    waits_alone(sp)
                    sp.dma_start(x_out[c.n], x_new[c.parity][:]).then_inc(s_store[c.parity], 16)

            run_slots(sp, slot, 4, NT + 2)
            for i in range(2):
                sp.wait_ge(s_store[i], 16 * NT // 2)

        @block.gpsimd
        def _(pool):
            nc.gpsimd.memset(minus_half[:], -0.5).then_inc(s_init, 1)
            for i in range(2):
                nc.gpsimd.memset(Vb[i][:], 0.0).then_inc(s_init, 1)
            pool.wait_ge(s_init, 3)
            if not rope:
                pool.wait_ge(s_const, 16 * len(const_loads))
                nc.gpsimd.tensor_scalar(bqk[:, 0], bqk[:, 0], d_head ** -0.5, None, ALU.mult).then_inc(s_bq, 1)
                pool.wait_ge(s_bq, 1)
            for i in range(2):
                for b in range(2):
                    col = b * (d_head + 1) + d_head
                    nc.gpsimd.memset(Vb[i][b * SEQ:(b + 1) * SEQ, :, :, col:col + 1], 1.0).then_inc(s_init, 1)
                    pool.wait_ge(s_init, 4 + 2 * i + b)
            pool.wait_ge(s_const, 16 * len(const_loads))

            def slot(u):
                v, c, i = u.back(1), u.back(3), u.parity
                if there(u):
                    pool.wait_ge(s_in[i], dmas(u, n_in))
                    if there(u.back(2)):
                        pool.wait_ge(s_vproj, nth(u.back(2), 1, 1))
                    waits_alone(pool)
                    raw = kvin[i] if rope else qin[i]
                    nc.gpsimd.tensor_copy(kv_hi[i][:], raw[:]).then_inc(s_split, 1)
                    pool.wait_ge(s_split, nth(u, 2, 1))
                    nc.gpsimd.tensor_tensor(kv_lo[i][:], raw[:], kv_hi[i][:].bitcast(F32),
                                            ALU.subtract).then_inc(s_split, 1)
                if rope and there(v):
                    cos = cs[v.parity][:, 0:1, :].to_broadcast([P, EC, TOK])
                    for o in range(2):
                        pool.wait_ge(s_plain, nth(v, 2, o + 1))
                        if there(v.back(1)):
                            pool.wait_ge(s_rot, nth(v.back(1), 2, o + 1))
                        nc.gpsimd.tensor_tensor(rot[:, o, 2], rot[:, o, 0], cos, ALU.mult).then_inc(s_cos, 1)
                        pool.wait_ge(s_rot, nth(v, 2, o + 1))
                        pool.wait_ge(s_hi, nth(v, 2, o + 1))
                        if there(v.back(1)):
                            pool.wait_ge(s_scr[o], v.n * 16)
                        nc.gpsimd.tensor_tensor(qk16[:, o, 1], rot[:, o, 1], qk16[:, o, 0],
                                                ALU.subtract).then_inc(s_lo, 1)
                if there(c):
                    i = c.parity
                    pool.wait_ge(s_tok[i], dmas(c, 1))
                    nc.gpsimd.tensor_tensor(tok_in[i][:], tok_in[i][:],
                                            bo_bc[:].rearrange("p (o n) -> p o n", o=1).to_broadcast([P, 2, E]),
                                            ALU.add).then_inc(s_xb, 1)
                    for pr in range(2):
                        pool.wait_ge(s_var, nth(c, 2, pr + 1))
                        waits_alone(pool)
                        nc.gpsimd.tensor_scalar(rstd[:, pr:pr + 1], mv[:, pr, 1:2], LN_EPS, None,
                                                ALU.add).then_inc(s_eps, 1)
                        pool.wait_ge(s_eps, nth(c, 2, pr + 1))
                        nc.gpsimd.tensor_tensor(rstd[:, pr:pr + 1], rstd[:, pr:pr + 1], minus_half[:],
                                                ALU.pow).then_inc(s_rstd, 1)
                        pool.wait_ge(s_rstd, nth(c, 2, pr + 1))
                        if pr == 0 and there(c.back(2)):
                            pool.wait_ge(s_store[i], dmas(c.back(2), 1))
                        waits_alone(pool)
                        nc.gpsimd.tensor_scalar(x_new[i][:, pr], y[:, pr], mv[:, pr, 0:1], rstd[:, pr:pr + 1],
                                                ALU.subtract, ALU.mult).then_inc(s_new, 1)

            run_slots(pool, slot, 6, NT + 2)

        @block.scalar
        def _(act):
            act.wait_ge(s_const, 16 * len(const_loads))
            if not rope:
                act.wait_ge(s_bq, 1)

            def high_parts(s, o):
                if there(s.back(1)):
                    act.wait_ge(s_scr[o], (s.n) * 16)
                if rope:
                    act.wait_ge(s_rot, nth(s, 2, o + 1))
                    nc.scalar.activation(qk16[:, o, 0], rot[:, o, 1], ACT.Copy).then_inc(s_hi, 1)
                    return
                act.wait_ge(s_qkproj, nth(s, 2, o + 1))
                for ch in range(EC):
                    nc.scalar.activation(qk16[:, o, 0, ch], psJ[o][:, bass.ts(ch, TOK)], ACT.Identity,
                                         bias=bqk[:, o, ch:ch + 1]).then_inc(s_hi, 1)

            def plain(s, o):
                act.wait_ge(s_qkproj, nth(s, 2, o + 1))
                if there(s.back(1)):
                    act.wait_ge(s_swap, nth(s.back(1), 2, o + 1))
                    act.wait_ge(s_cos, nth(s.back(1), 2, o + 1))
                nc.scalar.activation(rot[:, o, 0], psJ[o][:].rearrange("p (c n) -> p c n", c=EC), ACT.Copy,
                                     scale=1.0 if o else d_head ** -0.5).then_inc(s_plain, 1)

            def probs(c, k):
                pr, x = divmod(k, NX)
                act.wait_ge(s_xscore, nth(c, STEPS, k + 1))
                if there(c.back(1)):
                    act.wait_ge(s_pv, nth(c.back(1), 2, pr + 1))
                nc.scalar.activation(PT[pr][:, bass.ts(x, 512)], psX[k % 2][:], ACT.Exp).then_inc(s_exp, 1)

            def attn_high(c, pr):
                act.wait_ge(s_atr, nth(c, 2, pr + 1))
                if there(c.back(1)):
                    act.wait_ge(s_proj, nth(c.back(1), 2, pr + 1))
                nc.scalar.activation(aT_hi[:, pr].rearrange("p r (b q) -> p b r q", b=2), aT_ps(),
                                     ACT.Copy).then_inc(s_ahi, 1)

            def slot(s):
                b_, c = s.back(1), s.back(2)
                if there(s):
                    if rope:
                        act.wait_ge(s_xtr, nth(s, 1, 1))
                        nc.scalar.activation(q_hi[0][:], psM[0][:].rearrange("p (c n) -> p c n", c=EC),
                                             ACT.Copy).then_inc(s_xhi, 1)
                        plain(s, 0)
                    else:
                        high_parts(s, 0)
                if there(c):
                    for k in range(NX):
                        probs(c, k)
                if there(s):
                    if rope:
                        high_parts(s, 0)
                        plain(s, 1)
                    else:
                        high_parts(s, 1)
                if there(c):
                    for k in range(NX, STEPS):
                        probs(c, k)
                if there(s) and rope:
                    high_parts(s, 1)
                if there(c):
                    attn_high(c, 0)
                if there(b_):
                    act.wait_ge(s_mt, nth(b_, 1, 1))
                    act.dma_start(Q3[b_.parity][ROWS_M:ROWS_X], mT[:]).then_inc(s_mrow[b_.parity], 16)
                if there(c):
                    attn_high(c, 1)

            run_slots(act, slot, 4, NT + 1)

        @block.vector
        def _(dve):
            dve.wait_ge(s_const, 16 * len(const_loads))
            dve.wait_ge(s_init, 7)

            if not rope:
                nc.vector.tensor_copy(mask_q[:], mask_raw[:, 0]).then_inc(s_mask, 1)
                nc.vector.tensor_copy(mask_k[:], mask_raw[:, 1]).then_inc(s_mask, 1)
                nc.vector.tensor_copy(ident_bf[:], ident[:]).then_inc(s_mask, 1)

            def spread_q(s):
                i = s.parity
                dve.wait_ge(s_qr, nth(s, 48, 48))
                if there(s.back(2)):
                    dve.wait_ge(s_xscore, nth(s.back(2), STEPS, STEPS))
                for h in range(G):
                    nc.vector.tensor_scalar(Q3[i][0:SPLIT, :, :, bass.ts(h, SEQ)].rearrange("r g b q -> r (g b) q"),
                                            Qr[:].rearrange("r g (b q) -> r (g b) q", q=SEQ), head_rows[:, h:h + 1],
                                            None, ALU.mult).then_inc(s_q3, 1)

            def low_parts(s, o):
                dve.wait_ge(s_hi, nth(s, 4, 2 * o + 2))
                for ch in range(EC):
                    nc.vector.scalar_tensor_tensor(qk16[:, o, 1, ch], psJ[o][:, bass.ts(ch, TOK)],
                                                   bqk[:, o, ch:ch + 1], qk16[:, o, 0, ch],
                                                   ALU.add, ALU.subtract).then_inc(s_lo, 1)

            def swapped_by_sin(s, o):
                dve.wait_ge(s_plain, nth(s, 2, o + 1))
                if there(s.back(1)):
                    dve.wait_ge(s_lo, nth(s.back(1), 2, o + 1))
                    dve.wait_ge(s_hi, nth(s.back(1), 2, o + 1))
                waits_alone(dve)
                nc.vector.stream_shuffle(rot[:, o, 1], rot[:, o, 0], [n ^ 1 for n in range(32)]).then_inc(s_swap, 1)
                dve.wait_ge(s_swap, nth(s, 2, o + 1))
                nc.vector.tensor_tensor(rot[:, o, 1], rot[:, o, 1],
                                        cs[s.parity][:, 1:2, :].to_broadcast([P, EC, TOK]), ALU.mult).then_inc(s_sin, 1)

            def rotated(s, o):
                dve.wait_ge(s_sin, nth(s, 2, o + 1))
                dve.wait_ge(s_cos, nth(s, 2, o + 1))
                nc.vector.tensor_tensor(rot[:, o, 1], rot[:, o, 1], rot[:, o, 2], ALU.add).then_inc(s_rot, 1)

            def maxima(b_, m):
                dve.wait_ge(s_mscore, nth(b_, STEPS, m + 1))
                if m == 0 and there(b_.back(1)):
                    dve.wait_ge(s_mtr, nth(b_.back(1), 1, 1))
                nc.vector.tensor_reduce(mx[:, bass.ts(m, 8)], psM[m % 2][:].rearrange("p (c k) -> p c k", k=SEQ),
                                        AX_X, ALU.max).then_inc(s_mx, 1)

            def normalise(c, pr):
                dve.wait_ge(s_pv, nth(c, 2, pr + 1))
                o = po(pr)
                nc.vector.reciprocal(rec[:, pr], o[:, :, :, d_head:d_head + 1].rearrange("p h b e -> p h (b e)"))\
                    .then_inc(s_rec, 1)
                dve.wait_ge(s_rec, nth(c, 2, pr + 1))
                if there(c.back(1)):
                    dve.wait_ge(s_atr, nth(c.back(1), 2, pr + 1))
                nc.vector.tensor_tensor(
                    On[:, pr].rearrange("p b (h e) -> p b h e", e=d_head),
                    o[:, :, :, 0:d_head].rearrange("p h b e -> p b h e"),
                    rec[:, pr].rearrange("p h (b e) -> p b h e", e=1).to_broadcast([P, 2, heads // 2, d_head]),
                    ALU.mult).then_inc(s_on, 1)

            def attn_low(c, pr):
                dve.wait_ge(s_ahi, nth(c, 2, pr + 1))
                nc.vector.tensor_tensor(aT_lo[:, pr].rearrange("p r (b q) -> p b r q", b=2), aT_ps(),
                                        aT_hi[:, pr].bitcast(F32).rearrange("p r (b q) -> p b r q", b=2),
                                        ALU.subtract).then_inc(s_alo, 1)

            def place_v(s):
                dve.wait_ge(s_vproj, nth(s, 1, 1))
                for b in range(2):
                    rows = slice(b * SEQ, (b + 1) * SEQ)
                    out = Vb[s.parity][rows, :, :, b * (d_head + 1):b * (d_head + 1) + d_head]
                    v = psJ[0][rows, :].rearrange("p (r h e) -> p r h e", r=2, e=d_head)
                    if rope:
                        nc.vector.tensor_copy(out, v).then_inc(s_vb, 1)
                    else:
                        bias = bv_bc[rows, :].rearrange("p (r h e) -> p r h e", r=1, e=d_head)
                        nc.vector.tensor_tensor(out, v, bias.to_broadcast([SEQ, 2, heads, d_head]),
                                                ALU.add).then_inc(s_vb, 1)

            def residual(c, pr):
                dve.wait_ge(s_proj, nth(c, 2, pr + 1))
                dve.wait_ge(s_xb, nth(c, 1, 1))
                if there(c.back(1)):
                    dve.wait_ge(s_new, nth(c.back(1), 2, pr + 1))
                nc.vector.tensor_tensor(y[:, pr], psJ[1][:, 0:E], tok_in[c.parity][:, pr], ALU.add).then_inc(s_y, 1)
                dve.wait_ge(s_y, nth(c, 2, pr + 1))
                nc.vector.bn_stats(stats[:, pr], y[:, pr]).then_inc(s_stat, 1)
                dve.wait_ge(s_stat, nth(c, 2, pr + 1))
                waits_alone(dve)
                nc.vector.bn_aggr(mv[:, pr], stats[:, pr]).then_inc(s_var, 1)

            def slot(s):
                b_, c = s.back(1), s.back(2)
                if there(s):
                    if rope:
                        dve.wait_ge(s_xhi, nth(s, 1, 1))
                        nc.vector.tensor_tensor(q_lo[0][:], psM[0][:].rearrange("p (c n) -> p c n", c=EC),
                                                q_hi[0][:].bitcast(F32), ALU.subtract).then_inc(s_xlo, 1)
                        swapped_by_sin(s, 0)
                    else:
                        low_parts(s, 0)
                if there(b_):
                    for m in range(NX):
                        maxima(b_, m)
                if there(s):
                    if rope:
                        rotated(s, 0)
                        swapped_by_sin(s, 1)
                    else:
                        low_parts(s, 1)
                if there(c):
                    normalise(c, 0)
                if there(b_):
                    for m in range(NX, STEPS):
                        maxima(b_, m)
                if there(s) and rope:
                    rotated(s, 1)
                if there(c):
                    attn_low(c, 0)
                if there(b_):
                    dve.wait_ge(s_mtr, nth(b_, 1, 1))
                    if there(b_.back(1)):
                        dve.wait_ge(s_mrow[1 - b_.parity], dmas(b_.back(1), 1))
                    nc.vector.tensor_scalar(mT[:], psJ[1][0:MCOL, 0:P], M_CLAMP, -M_CLAMP,
                                            ALU.min, ALU.max).then_inc(s_mt, 1)
                if there(c):
                    normalise(c, 1)
                if there(s):
                    place_v(s)
                    spread_q(s)
                if there(c):
                    residual(c, 0)
                    attn_low(c, 1)
                    residual(c, 1)

            run_slots(dve, slot, 4, NT + 1)

        @block.tensor
        def _(pe):
            pe.wait_ge(s_const, 16 * len(const_loads))
            pe.wait_ge(s_init, 7)
            if not rope:
                pe.wait_ge(s_mask, 3)

            def qk_copied(s, o):
                if rope:
                    pe.wait_ge(s_plain, nth(s, 2, o + 1))
                else:
                    pe.wait_ge(s_lo, nth(s, 4, 2 * o + 2))

            def project(s, o):
                w, hi, lo = (wk, kv_hi, kv_lo) if o else (wq, q_hi, q_lo)
                x_hi, x_lo = (hi[s.parity], lo[s.parity]) if o or not rope else (hi[0], lo[0])
                n_k = KC if o else EC
                for ch in range(EC):
                    for k in range(n_k):
                        last = mm3(nc, psJ[o][:, bass.ts(ch, TOK)], w[0][:, k, bass.ts(ch, P)],
                                   w[1][:, k, bass.ts(ch, P)], x_hi[:, k], x_lo[:, k], k == 0, k == n_k - 1)
                last.then_inc(s_qkproj, 1)

            def max_scores(b_, m):
                if m or there(b_.back(1)):
                    if not (m == 1 and not there(b_.back(1))):
                        pe.wait_ge(s_mx, nth(b_, STEPS, m - 1))
                if m == 0:
                    pe.wait_ge(s_q3, nth(b_, G, G))
                    pe.wait_ge(s_k3[b_.parity], dmas(b_, 3))
                out, i = psM[m % 2], b_.parity
                if not rope:
                    nc.tensor.matmul(out[:], ident_bf[:], mask_q[:], start=True, stop=True, skip_group_check=True)
                for k in range(8):
                    g, b, a = (m * 8 + k) // (BPT * G // 2), (m * 8 + k) // (G // 2) % BPT, k % (G // 2)
                    last = nc.tensor.matmul(out[:, bass.ts(k, SEQ)], Q3[i][0:ROWS_M, g, b, bass.ts(a, P)],
                                            K3[i][0:ROWS_M, g, i_chunk[b]], start=rope and k == 0, stop=True,
                                            skip_group_check=True)
                last.then_inc(s_mscore, 1)

            def scores(c, k):
                pr, x = divmod(k, NX)
                i, out = c.parity, psX[k % 2]
                if k > 1 or there(c.back(1)):
                    pe.wait_ge(s_exp, nth(c, STEPS, k - 1))
                if k == 0:
                    pe.wait_ge(s_mrow[i], dmas(c, 1))
                if not rope:
                    nc.tensor.matmul(out[:], ident_bf[:], mask_k[:], start=True, stop=True, skip_group_check=True)
                n_g = 8 // G
                for b in range(2):
                    for n in range(n_g):
                        g, b4 = x * n_g + n, 2 * pr + b
                        last = nc.tensor.matmul(out[b * SEQ:(b + 1) * SEQ, bass.ts(n, G * SEQ)],
                                                K3[i][0:ROWS_X, g, i_chunk[b4]], Q3[i][0:ROWS_X, g, b4],
                                                start=rope and n == 0, stop=True, skip_group_check=True)
                last.then_inc(s_xscore, 1)

            def attend(c, pr):
                if POB == 1:
                    if there(c.back(1)):
                        pe.wait_ge(s_on, nth(c.back(1), 2, pr + 1))
                elif pr or there(c.back(1)):
                    pe.wait_ge(s_on, nth(c, 2, pr))
                pe.wait_ge(s_vb, nth(c, 2, 2))
                for h in range(heads):
                    if h % 8 == 0:
                        pe.wait_ge(s_exp, nth(c, STEPS, pr * NX + h // 8 + 1))
                    bank, col = divmod(h // 2, 512 // VW)
                    last = nc.tensor.matmul(psO[(h % 2) * SEQ:(h % 2 + 1) * SEQ, pr if POB == 1 else bank,
                                                bass.ts(col, VW)],
                                            PT[pr][:, bass.ts(h, SEQ)], Vb[c.parity][:, pr, h, :],
                                            start=True, stop=True, skip_group_check=True)
                last.then_inc(s_pv, 1)

            def transpose_attn(c, pr):
                pe.wait_ge(s_on, nth(c, 2, pr + 1))
                for b in range(2):
                    last = nc.tensor.transpose(psJ[0][:, bass.ts(b, P)], On[:, pr, b], ident[:])
                last.then_inc(s_atr, 1)

            def project_out(c, pr):
                pe.wait_ge(s_alo, nth(c, 2, pr + 1))
                for r in range(2):
                    last = mm3(nc, psJ[1][:, 0:E], aT_hi[:, pr, r], aT_lo[:, pr, r], wo[0][:, r], wo[1][:, r],
                               r == 0, r == 1)
                last.then_inc(s_proj, 1)

            def slot(s):
                b_, c, d = s.back(1), s.back(2), s.back(3)
                if there(s):
                    if rope:
                        pe.wait_ge(s_in[s.parity], dmas(s, n_in))
                        if there(c):
                            pe.wait_ge(s_mx, nth(c, STEPS, STEPS - 1))
                        elif there(b_):
                            pe.wait_ge(s_xlo, nth(b_, 1, 1))
                        if there(b_):
                            pe.wait_ge(s_qkproj, nth(b_, 2, 2))
                        for r in range(2):
                            for ch in range(EC):
                                last = nc.tensor.transpose(psM[0][:, ch * TOK + r * P:ch * TOK + (r + 1) * P],
                                                           tok_a[s.parity][:, r, bass.ts(ch, P)], ident[:])
                        last.then_inc(s_xtr, 1)
                        pe.wait_ge(s_xlo, nth(s, 1, 1))
                    else:
                        pe.wait_ge(s_split, nth(s, 2, 2))
                    if there(d):
                        pe.wait_ge(s_alo, nth(d, 2, 2))
                    if there(b_):
                        pe.wait_ge(s_vb, nth(b_, 2, 2))
                    project(s, 0)
                for k in range(NX):
                    if there(c):
                        scores(c, k)
                    if there(b_):
                        max_scores(b_, k)
                if there(s):
                    if rope:
                        pe.wait_ge(s_split, nth(s, 2, 2))
                    if there(d):
                        pe.wait_ge(s_y, nth(d, 2, 2))
                    if there(c):
                        pe.wait_ge(s_mt, nth(c, 1, 1))
                    if there(b_):
                        qk_copied(b_, 1)
                    project(s, 1)
                if there(c):
                    attend(c, 0)
                for k in range(NX, STEPS):
                    if there(c):
                        scores(c, k)
                    if there(b_):
                        max_scores(b_, k)
                if there(c):
                    if there(s):
                        qk_copied(s, 0)
                    transpose_attn(c, 0)
                if there(b_):
                    if there(s):
                        qk_copied(s, 1)
                    if there(d):
                        pe.wait_ge(s_y, nth(d, 2, 2))
                    pe.wait_ge(s_mx, nth(b_, STEPS, STEPS))
                    waits_alone(pe)
                    nc.tensor.transpose(psJ[1][0:MCOL, 0:P], mx[:], ident[:]).then_inc(s_mtr, 1)
                if there(c):
                    attend(c, 1)
                if there(s):
                    qk_copied(s, 0)
                    if there(c):
                        pe.wait_ge(s_alo, nth(c, 2, 1))
                    for pr in range(2):
                        for k in range(KC):
                            x = bass.ts(pr, P)
                            last = mm3(nc, psJ[0][:, bass.ts(pr, E)], kv_hi[s.parity][:, k, x], kv_lo[s.parity][:, k, x],
                                       wv[0][:, k], wv[1][:, k], k == 0, k == KC - 1)
                    last.then_inc(s_vproj, 1)
                if there(c):
                    if there(b_):
                        pe.wait_ge(s_mt, nth(b_, 1, 1))
                    elif there(d):
                        pe.wait_ge(s_y, nth(d, 2, 2))
                    project_out(c, 0)
                    if there(s):
                        pe.wait_ge(s_vb, nth(s, 2, 2))
                    transpose_attn(c, 1)
                    pe.wait_ge(s_y, nth(c, 2, 1))
                    project_out(c, 1)

            run_slots(pe, slot, 4, NT + 1)


def ffn(nc, x_in, w_dram, out, consts):
    FT = 4
    N = FT * P
    NTF = NSEQ * SEQ // N
    HC = HID // P

    with ExitStack() as ctx:
        def sb(name, shape, dt):
            return ctx.enter_context(nc.sbuf_tensor(f"f_{name}", shape, dt))

        def ps(name, shape):
            return ctx.enter_context(nc.psum_tensor(f"f_{name}", shape, F32))

        def sem(name):
            return ctx.enter_context(nc.semaphore(f"f_{name}"))

        wg = [sb(f"wg{i}", [P, EC, HID], F32R) for i in range(2)]
        wu = [sb(f"wu{i}", [P, EC, HID], F32R) for i in range(2)]
        wd = [sb(f"wd{i}", [P, HC, E], F32R) for i in range(2)]
        with ExitStack() as raw_ctx:
            raws = [raw_ctx.enter_context(nc.sbuf_tensor(f"f_raw{i}", shape, F32))
                    for i, shape in enumerate(([P, EC, HID], [P, EC, HID], [P, HC, E]))]
            split_weights(nc, [(w_dram[n], r[:], w[0][:], w[1][:], 1.0)
                               for n, r, w in zip(("wg", "wu", "wd"), raws, (wg, wu, wd))])

        x_tok = [sb(f"x_tok{i}", [P, FT, E], F32) for i in range(2)]
        x_res = [sb(f"x_res{i}", [P, FT, E], F32) for i in range(2)]
        x_hi, x_lo = sb("x_hi", [P, EC, N], F32R), sb("x_lo", [P, EC, N], F32R)
        gate = [sb(f"gate{i}", [P, N], F32) for i in range(2)]
        hid = [sb(f"hid{i}", [P, N], F32) for i in range(2)]
        h_hi = [sb(f"h_hi{i}", [P, HC, N], F32R) for i in range(2)]
        h_lo = [sb(f"h_lo{i}", [P, HC, N], F32R) for i in range(2)]
        y = sb("y", [P, FT, E], F32)
        stats = sb("stats", [P, FT, 6], F32)
        mv = sb("mv", [P, FT, 2], F32)
        rstd = sb("rstd", [P, FT], F32)
        x_new = [sb(f"xn{i}", [P, FT, E], F32) for i in range(2)]
        minus_half = sb("mh", [P, FT], F32)
        ident = sb("ident", [P, P], F32)

        psT = [ps(f"psT{i}", [P, N]) for i in range(2)]
        psG = [ps(f"psG{i}", [P, N]) for i in range(2)]
        psU = [ps(f"psU{i}", [P, N]) for i in range(2)]
        psD = [ps(f"psD{i}", [P, 2, E]) for i in range(2)]

        s_const = sem("const_loaded")
        s_init = sem("constants_set")
        s_in = [sem(f"in_loaded{i}") for i in range(2)]
        s_res = [sem(f"res_loaded{i}") for i in range(2)]
        s_xtr = sem("input_transposed")
        s_xhi = sem("input_high")
        s_xlo = sem("input_low")
        s_gate = sem("gate_done")
        s_up = sem("up_done")
        s_silu = sem("silu_done")
        s_h = sem("hidden_done")
        s_hhi = sem("hidden_high")
        s_hlo = sem("hidden_low")
        s_down = sem("down_done")
        s_y = sem("residual_added")
        s_stat = sem("stats_done")
        s_var = sem("variance_done")
        s_eps = sem("eps_added")
        s_rstd = sem("rstd_done")
        s_new = sem("normed")
        s_store = [sem(f"out_stored{i}") for i in range(2)]
        block = ctx.enter_context(nc.Block())

        def is_tile(t):
            return there(t, NTF)

        @block.sync
        def _(sp):
            sp.dma_start(ident[:], consts["ident"]).then_inc(s_const, 16)

            def slot(u):
                v, c, i = u.back(1), u.back(2), u.parity
                if is_tile(u):
                    if is_tile(c):
                        sp.wait_ge(s_xtr, nth(c, 1, 1))
                        waits_alone(sp)
                    sp.dma_start(x_tok[i][:].rearrange("p (a r) e -> p a r e", a=2), x_in[u.n])\
                        .then_inc(s_in[i], 16)
                if is_tile(v):
                    if is_tile(v.back(2)):
                        sp.wait_ge(s_y, nth(v.back(2), 2, 2))
                        waits_alone(sp)
                    sp.dma_start(x_res[1 - i][:].rearrange("p (a r) e -> p a r e", a=2), x_in[v.n])\
                        .then_inc(s_res[1 - i], 16)
                if is_tile(c):
                    sp.wait_ge(s_new, nth(c, FT, FT))
                    waits_alone(sp)
                    sp.dma_start(out[c.n], x_new[i][:]).then_inc(s_store[i], 16)

            run_slots(sp, slot, 4, NTF + 1, NTF)
            for i in range(2):
                sp.wait_ge(s_store[i], 16 * NTF // 2)

        @block.scalar
        def _(act):
            def slot(s):
                if not is_tile(s):
                    return
                for ch in range(EC):
                    act.wait_ge(s_xtr, nth(s, 1, 1))
                    if is_tile(s.back(1)):
                        act.wait_ge(s_up, nth(s.back(1), HC, HC))
                    nc.scalar.activation(x_hi[:, ch], psT[ch][:], ACT.Copy).then_inc(s_xhi, 1)
                for h in range(HC):
                    b = h % 2
                    act.wait_ge(s_gate, nth(s, HC, h + 1))
                    if h > 1 or is_tile(s.back(1)):
                        act.wait_ge(s_h, nth(s, HC, h - 1))
                    nc.scalar.activation(gate[b][:], psG[b][:], ACT.Silu).then_inc(s_silu, 1)
                    act.wait_ge(s_h, nth(s, HC, h + 1))
                    if is_tile(s.back(2)):
                        act.wait_ge(s_down, nth(s.back(2), FT, FT))
                    nc.scalar.activation(h_hi[s.parity][:, h], hid[b][:], ACT.Copy).then_inc(s_hhi, 1)

            run_slots(act, slot, 4, NTF - 1, NTF)

        @block.vector
        def _(dve):
            def slot(s):
                c = s.back(1)
                if is_tile(s):
                    for ch in range(EC):
                        dve.wait_ge(s_xhi, nth(s, EC, ch + 1))
                        nc.vector.tensor_tensor(x_lo[:, ch], psT[ch][:], x_hi[:, ch].bitcast(F32),
                                                ALU.subtract).then_inc(s_xlo, 1)
                for h in range(HC):
                    b = h % 2
                    if is_tile(s):
                        dve.wait_ge(s_silu, nth(s, HC, h + 1))
                        dve.wait_ge(s_up, nth(s, HC, h + 1))
                        if h > 1 or is_tile(s.back(1)):
                            dve.wait_ge(s_hlo, nth(s, HC, h - 1))
                        nc.vector.tensor_tensor(hid[b][:], gate[b][:], psU[b][:], ALU.mult).then_inc(s_h, 1)
                    if is_tile(c) and h in (4, 7):
                        half = h // 7
                        dve.wait_ge(s_down, nth(c, FT, 2 * half + 2))
                        dve.wait_ge(s_res[c.parity], dmas(c, 1))
                        if is_tile(c.back(1)):
                            dve.wait_ge(s_new, nth(c.back(1), FT, 2 * half + 2))
                        nc.vector.tensor_tensor(y[:, 2 * half:2 * half + 2], psD[half][:],
                                                x_res[c.parity][:, 2 * half:2 * half + 2], ALU.add).then_inc(s_y, 1)
                        dve.wait_ge(s_y, nth(c, 2, half + 1))
                        for r in range(2 * half, 2 * half + 2):
                            nc.vector.bn_stats(stats[:, r], y[:, r]).then_inc(s_stat, 1)
                        dve.wait_ge(s_stat, nth(c, FT, 2 * half + 2))
                        waits_alone(dve)
                        for r in range(2 * half, 2 * half + 2):
                            nc.vector.bn_aggr(mv[:, r], stats[:, r]).then_inc(s_var, 1)

            run_slots(dve, slot, 4, NTF, NTF)

        @block.gpsimd
        def _(pool):
            nc.gpsimd.memset(minus_half[:], -0.5).then_inc(s_init, 1)
            pool.wait_ge(s_init, 1)

            def slot(s):
                c = s.back(1)
                for h in range(HC):
                    if is_tile(s):
                        pool.wait_ge(s_hhi, nth(s, HC, h + 1))
                        nc.gpsimd.tensor_tensor(h_lo[s.parity][:, h], hid[h % 2][:],
                                                h_hi[s.parity][:, h].bitcast(F32), ALU.subtract).then_inc(s_hlo, 1)
                    if is_tile(c) and h in (5, 7):
                        half = h // 7
                        rows = slice(2 * half, 2 * half + 2)
                        pool.wait_ge(s_var, nth(c, FT, 2 * half + 2))
                        waits_alone(pool)
                        nc.gpsimd.tensor_scalar(rstd[:, rows], mv[:, rows, 1:2].rearrange("p r e -> p (r e)"), LN_EPS,
                                                None, ALU.add).then_inc(s_eps, 1)
                        pool.wait_ge(s_eps, nth(c, 2, half + 1))
                        nc.gpsimd.tensor_tensor(rstd[:, rows], rstd[:, rows], minus_half[:, rows],
                                                ALU.pow).then_inc(s_rstd, 1)
                        pool.wait_ge(s_rstd, nth(c, 2, half + 1))
                        if half == 0 and is_tile(c.back(2)):
                            pool.wait_ge(s_store[c.parity], dmas(c.back(2), 1))
                        waits_alone(pool)
                        for r in range(2 * half, 2 * half + 2):
                            nc.gpsimd.tensor_scalar(x_new[c.parity][:, r], y[:, r], mv[:, r, 0:1], rstd[:, r:r + 1],
                                                    ALU.subtract, ALU.mult).then_inc(s_new, 1)

            run_slots(pool, slot, 4, NTF, NTF)

        @block.tensor
        def _(pe):
            pe.wait_ge(s_const, 16)

            def slot(s):
                c = s.back(1)
                if is_tile(s):
                    pe.wait_ge(s_in[s.parity], dmas(s, 1))
                    if is_tile(c):
                        pe.wait_ge(s_xlo, nth(c, EC, EC))
                    for ch in range(EC):
                        for r in range(FT):
                            last = nc.tensor.transpose(psT[ch][:, bass.ts(r, P)], x_tok[s.parity][:, r, bass.ts(ch, P)],
                                                       ident[:])
                    last.then_inc(s_xtr, 1)
                    pe.wait_ge(s_xlo, nth(s, EC, EC))
                for h in range(HC):
                    if is_tile(s):
                        if h > 1 or is_tile(c):
                            pe.wait_ge(s_silu, nth(s, HC, h - 1))
                            pe.wait_ge(s_h, nth(s, HC, h - 1))
                        for w, bank, done in ((wg, psG[h % 2], s_gate), (wu, psU[h % 2], s_up)):
                            for k in range(EC):
                                last = mm3(nc, bank[:], w[0][:, k, bass.ts(h, P)], w[1][:, k, bass.ts(h, P)],
                                           x_hi[:, k], x_lo[:, k], k == 0, k == EC - 1)
                            last.then_inc(done, 1)
                    if is_tile(c) and h % 2:
                        r = h // 2
                        if r == 0:
                            pe.wait_ge(s_hlo, nth(c, HC, HC))
                        if is_tile(c.back(1)):
                            pe.wait_ge(s_y, nth(c.back(1), 2, r // 2 + 1))
                        for k in range(HC):
                            x = bass.ts(r, P)
                            last = mm3(nc, psD[r // 2][:, r % 2], h_hi[c.parity][:, k, x], h_lo[c.parity][:, k, x],
                                       wd[0][:, k], wd[1][:, k], k == 0, k == HC - 1)
                        last.then_inc(s_down, 1)

            run_slots(pe, slot, 4, NTF, NTF)


def decoder_layer(nc, a, out, stages=3):
    x1 = nc.dram_tensor("x1", [NT, P, 2, E], F32, kind="Internal").ap()
    x2 = nc.dram_tensor("x2", [NT, P, 2, E], F32, kind="Internal").ap()
    cs = nc.dram_tensor("cos_sin", [2, P, NSEQ * SEQ], F32, kind="Internal").ap()
    scratch = nc.dram_tensor("split_parts", [2, 2, E // NG, NG // EC, 2, EC * TOK], F16, kind="Internal").ap()
    scratch_x = nc.dram_tensor("split_parts_x", [2, 2, E // NG, NG // EC, 2, EC * TOK], F16, kind="Internal").ap()

    def chunks(w):
        return w.rearrange("(k p) n -> p k n", p=P)

    rotary_tables(nc, a["pos"], a["rot_cols"], cs)
    attention(nc, 16, 16, False,
              {"tok": a["x_tok"].rearrange("(t r p) e -> t p r e", r=2, p=P), "T": chunks(a["x_T"])}, None,
              {n: chunks(a["s_" + n]) for n in ("wq", "wk", "wv", "wo")},
              x1 if stages > 1 else out.rearrange("(t r p) e -> t p r e", r=2, p=P),
              {"scratch": scratch, **{n: a[n] for n in ("ident", "mask_q", "mask_k", "q_rows", "head_rows")},
               "bo": a["s_bo"], "bv": a["s_bv"], "bqk": a["s_bqk"], "k_rows": a["s_k_rows"]})
    if stages < 2:
        return
    attention(nc, 32, 8, True, {"tok": x1}, chunks(a["ctx_T"]),
              {n: chunks(a["x_" + n]) for n in ("wq", "wk", "wv", "wo")},
              x2 if stages > 2 else out.rearrange("(t r p) e -> t p r e", r=2, p=P),
              {"scratch": scratch_x, "ident": a["ident"], "head_rows": a["x_head_rows"], "bo": a["x_bo"], "k_rows": a["x_k_rows"],
               "cs": cs.rearrange("a p n -> p a n")})
    if stages < 3:
        return
    ffn(nc, x2.rearrange("(t a) p r e -> t p a r e", a=2),
        {"wg": chunks(a["wg"]), "wu": chunks(a["wu"]), "wd": chunks(a["wd"])},
        out.rearrange("(t r p) e -> t p r e", r=4, p=P), {"ident": a["ident"]})


def layout(inputs):
    import numpy as np

    g = {k: np.asarray(v) for k, v in inputs.items()}
    copy = np.ascontiguousarray

    def rows(b):
        return copy(np.broadcast_to(b, (P, b.shape[0])))

    def out_weights(w, d):
        return copy(w.reshape(E // d // 2, 2, d, E).transpose(1, 0, 2, 3).reshape(E, E))

    def split16(v):
        hi = v.astype(np.float16)
        return hi, (v - hi.astype(np.float64)).astype(np.float16)

    def grouped(w, d):
        lead = w.shape[:-1]
        return copy(np.moveaxis(w.reshape(*lead, NG // EC, EC, E // NG), -2, -3).reshape(*lead, E))

    def head_rows(d):
        rows_of = np.arange(3 * E // NG) % (E // NG) // d
        return copy((rows_of[:, None] == np.arange(E // NG // d)).astype(np.float32))

    x = g["x"].reshape(-1, E)
    pos = g["fside_BxSx2_0"].reshape(-1, 2)
    channel = np.arange(P) % 8
    a = {
        "x_tok": copy(x), "x_T": copy(x.T),
        "ctx_T": copy(g["ctx_1024"].reshape(-1, CTX).T),
        "pos": copy(pos.T[channel // 4]),
        "s_wq": grouped(g["L0_attn_Wq"].T, 16), "s_wk": grouped(g["L0_attn_Wk"].T, 16), "s_wv": copy(g["L0_attn_Wv"].T),
        "s_wo": out_weights(copy(g["L0_attn_Wo"].T), 16),
        "s_bqk": copy(np.stack([grouped(g[n], 16).reshape(EC, P).T for n in ("L0_attn_bq", "L0_attn_bk")], 1)),
        "s_bv": rows(g["L0_attn_bv"]), "s_bo": rows(g["L0_attn_bo"]),
        "x_wq": grouped(g["L0_xattn_Wq"], 8), "x_wk": grouped(g["L0_xattn_Wkv"][:, :E], 8), "x_wv": copy(g["L0_xattn_Wkv"][:, E:]),
        "x_wo": out_weights(g["L0_xattn_Wout"], 8), "x_bo": rows(g["L0_xattn_bout"]),
        "wg": copy(g["L0_ffn_w_gate"].T), "wu": copy(g["L0_ffn_w_up"].T), "wd": copy(g["L0_ffn_w_down"].T),
    }
    freqs = (np.float32(10000.0) ** (-np.arange(2, dtype=np.float32) / np.float32(2))).astype(np.float32)
    a["rot_cols"] = np.stack([freqs[channel % 4 // 2], np.where(channel % 2, 1.0, -1.0)], 1).astype(np.float32)
    a["ident"] = np.eye(P, dtype=np.float32)
    i = np.arange(P)[:, None] % SEQ
    j = np.arange(512)[None] % SEQ
    a["mask_q"] = np.where(j > i, -1e30, 0.0).astype(np.float32)
    a["mask_k"] = np.where(i > j, -1e30, 0.0).astype(np.float32)
    start = 2.0 ** -0.5
    slopes = np.array([start * start ** h for h in range(16)], np.float32).astype(np.float64)
    at = np.arange(TOK) % SEQ
    hi, lo = split16(slopes.reshape(NG, 2, 1) * at)
    one = np.ones((NG, TOK), np.float16)
    a["s_k_rows"] = copy(np.stack([hi[:, 0], lo[:, 0], hi[:, 1], lo[:, 1], one, one, -one]))
    q_rows = np.zeros((SELF_CONST, NG, BPT, 2, SEQ), np.float16)
    q_rows[0:2, :, :, 0] = 1
    q_rows[2:4, :, :, 1] = 1
    q_rows[4] = -hi[:, :, :SEQ][:, None]
    q_rows[5] = -lo[:, :, :SEQ][:, None]
    a["q_rows"] = q_rows.reshape(SELF_CONST, NG, BPT, 2 * SEQ)
    a["x_k_rows"] = copy(-one[None])
    a["head_rows"], a["x_head_rows"] = head_rows(16), head_rows(8)
    return a


def kernel(**inputs):
    import numpy as np
    from concourse import bacc
    from concourse.bass_utils import run_bass_kernel_spmd

    nc = bacc.Bacc("TRN2", target_bir_lowering=False, num_devices=1)
    arrays = layout(inputs)
    args = {n: nc.dram_tensor(f"in_{n}", v.shape, mybir.dt.from_np(v.dtype), kind="ExternalInput").ap()
            for n, v in arrays.items()}
    out = nc.dram_tensor("out", [NSEQ * SEQ, E], F32, kind="ExternalOutput").ap()
    decoder_layer(nc, args, out)
    got = run_bass_kernel_spmd(nc, [{f"in_{n}": v for n, v in arrays.items()}], core_ids=[0]).results[0]["out"]
    return np.asarray(got).reshape(NSEQ, SEQ, E)
```

```python
from contextlib import ExitStack

import concourse.bass as bass
from concourse import mybir

F32 = mybir.dt.float32
F32R = mybir.dt.float32r
F16 = mybir.dt.float16
BF16 = mybir.dt.bfloat16
ALU = mybir.AluOpType
ACT = mybir.ActivationFunctionType
AX_X = mybir.AxisListType.X

P = 128
SEQ = 64
NSEQ = 64
E = 256
CTX = 128
HID = 1024
TOK = 256
NT = NSEQ * SEQ // TOK
BPT = TOK // SEQ
NG = 8
EC = E // P
VW = 64
LN_EPS = 1e-5
M_CLAMP = 60000.0
SELF_CONST = 6
TWO_PI = (6.28125, 0.0019350051879882812, 3.0199159819149963e-07)
INV_TWO_PI = 0.15915494309189535
ROUND = 12582912.0
PI_IN = 3.1415925
HALF_PI = 1.5707963267948966


class Tile:

    def __init__(self, turn, parity):
        self.turn, self.parity = turn, parity
        self.n = turn * 2 + parity

    def back(self, k):
        m = self.parity - k
        return Tile(self.turn + m // 2 if m >= 0 else self.turn - (-m + 1) // 2, m % 2)


def there(t, tiles=NT):
    return not isinstance(t.n, int) or 0 <= t.n < tiles


def nth(t, per_tile, k):
    return t.n * per_tile + k


def dmas(t, count):
    return (t.turn + 1) * (16 * count)


def waits_alone(eng):
    eng.nop(nofuse=True)


def run_slots(eng, slot, loop_from, last, tiles=NT, first=0):
    def peeled(slots):
        for s in slots:
            slot(Tile(s // 2, s % 2))

    peeled(range(first, loop_from))
    with eng.Fori(loop_from // 2, tiles // 2 - 1) as turn:
        for parity in range(2):
            slot(Tile(turn, parity))
    peeled(range(tiles - 2, last + 1))


def mm3(nc, out, w_hi, w_lo, x_hi, x_lo, first, last):
    nc.tensor.matmul(out, w_hi, x_hi, start=first, stop=False)
    nc.tensor.matmul(out, w_hi, x_lo, start=False, stop=False)
    return nc.tensor.matmul(out, w_lo, x_hi, start=False, stop=last)


def split_weights(nc, parts):
    with nc.semaphore("w_loaded") as loaded, nc.semaphore("w_scaled") as scaled, \
            nc.semaphore("w_hi_done") as hi_done, nc.semaphore("w_lo_done") as lo_done, nc.Block() as block:
        @block.sync
        def _(sp):
            for dram, raw, _, _, _ in parts:
                sp.dma_start(raw, dram).then_inc(loaded, 16)

        @block.vector
        def _(dve):
            dve.wait_ge(loaded, 16 * len(parts))
            for n, (_, raw, hi, lo, scale) in enumerate(parts):
                nc.vector.tensor_scalar(raw, raw, scale, None, ALU.mult).then_inc(scaled, 1)
                dve.wait_ge(scaled, n + 1)
                nc.vector.tensor_copy(hi, raw).then_inc(hi_done, 1)
                dve.wait_ge(hi_done, n + 1)
                nc.vector.tensor_tensor(lo, raw, hi.bitcast(F32), ALU.subtract).then_inc(lo_done, 1)
            dve.wait_ge(lo_done, len(parts))


def rotary_tables(nc, pos_dram, cols_dram, cs_dram):
    n = NSEQ * SEQ
    with ExitStack() as ctx:
        def sb(name, shape, dt):
            return ctx.enter_context(nc.sbuf_tensor(f"r_{name}", shape, dt))

        pos = sb("pos", [P, n], F32)
        turns = sb("turns", [P, n], F32)
        cos_arg = sb("cos_arg", [P, n], F32)
        cols = sb("cols", [P, 2], F32)
        loaded = ctx.enter_context(nc.semaphore("r_loaded"))
        step = ctx.enter_context(nc.semaphore("r_step"))
        sined = ctx.enter_context(nc.semaphore("r_sined"))
        stored = ctx.enter_context(nc.semaphore("r_stored"))
        block = ctx.enter_context(nc.Block())

        @block.sync
        def _(sp):
            sp.dma_start(pos[:], pos_dram).then_inc(loaded, 16)
            sp.dma_start(cols[:], cols_dram).then_inc(loaded, 16)
            sp.wait_ge(sined, 2)
            sp.dma_start(cs_dram[0], cos_arg[:]).then_inc(stored, 16)
            sp.wait_ge(step, 10)
            sp.dma_start(cs_dram[1], pos[:]).then_inc(stored, 16)
            sp.wait_ge(stored, 32)

        @block.vector
        def _(dve):
            dve.wait_ge(loaded, 32)
            nc.vector.tensor_scalar(pos[:], pos[:], cols[:, 0:1], None, ALU.mult).then_inc(step, 1)
            dve.wait_ge(step, 1)
            nc.vector.tensor_scalar(turns[:], pos[:], INV_TWO_PI, ROUND, ALU.mult, ALU.add).then_inc(step, 1)
            dve.wait_ge(step, 2)
            nc.vector.tensor_scalar(turns[:], turns[:], ROUND, None, ALU.subtract).then_inc(step, 1)
            for k, part in enumerate(TWO_PI):
                dve.wait_ge(step, 3 + k)
                nc.vector.scalar_tensor_tensor(pos[:], turns[:], -part, pos[:], ALU.mult, ALU.add).then_inc(step, 1)
            dve.wait_ge(step, 6)
            nc.vector.tensor_scalar(pos[:], pos[:], PI_IN, -PI_IN, ALU.min, ALU.max).then_inc(step, 1)
            dve.wait_ge(step, 7)
            nc.vector.scalar_tensor_tensor(cos_arg[:], pos[:], -1.0, pos[:], ALU.mult, ALU.max).then_inc(step, 1)
            dve.wait_ge(step, 8)
            nc.vector.tensor_scalar(cos_arg[:], cos_arg[:], -1.0, HALF_PI, ALU.mult, ALU.add).then_inc(step, 1)
            dve.wait_ge(sined, 1)
            nc.vector.tensor_scalar(pos[:], pos[:], cols[:, 1:2], None, ALU.mult).then_inc(step, 1)

        @block.scalar
        def _(act):
            act.wait_ge(step, 9)
            nc.scalar.activation(pos[:], pos[:], ACT.Sin).then_inc(sined, 1)
            nc.scalar.activation(cos_arg[:], cos_arg[:], ACT.Sin).then_inc(sined, 1)


def attention(nc, heads, d_head, rope, src, kv_src, w_dram, x_out, consts):
    G = heads // NG
    SPLIT = 3 * d_head * G
    CONST = 0 if rope else SELF_CONST
    ROWS_M = SPLIT + CONST
    ROWS_X = ROWS_M + 1
    NX = heads * SEQ // 512
    MCOL = NG * BPT * G // 2
    OW = 28 if rope else VW
    KC = 1 if rope else EC
    pre = "x" if rope else "s"

    with ExitStack() as ctx:
        def sb(name, shape, dt):
            return ctx.enter_context(nc.sbuf_tensor(f"{pre}_{name}", shape, dt))

        def ps(name, shape):
            return ctx.enter_context(nc.psum_tensor(f"{pre}_{name}", shape, F32))

        def sem(name):
            return ctx.enter_context(nc.semaphore(f"{pre}_{name}"))

        wq = [sb(f"wq{i}", [P, EC, E], F32R) for i in range(2)]
        wk = [sb(f"wk{i}", [P, KC, E], F32R) for i in range(2)]
        wv = [sb(f"wv{i}", [P, KC, E], F32R) for i in range(2)]
        wo = [sb(f"wo{i}", [P, EC, E], F32R) for i in range(2)]
        with ExitStack() as raw_ctx:
            raws = [raw_ctx.enter_context(nc.sbuf_tensor(f"{pre}_raw{i}", [P, k, E], F32))
                    for i, k in enumerate((EC, KC, KC, EC))]
            q_scale = 1.0 if rope else d_head ** -0.5
            split_weights(nc, [(w_dram[n], r[:], w[0][:], w[1][:], q_scale if n == "wq" else 1.0)
                               for n, r, w in zip(("wq", "wk", "wv", "wo"), raws, (wq, wk, wv, wo))])

        qin = None if rope else [sb(f"qin{i}", [P, EC, TOK], F32) for i in range(2)]
        kvin = [sb(f"kvin{i}", [P, KC, TOK], F32) for i in range(2)] if rope else None
        tok_in = [sb(f"tok{i}", [P, 2, E], F32) for i in range(2)]
        tok_a = [sb(f"toka{i}", [P, 2, E], F32) for i in range(2)] if rope else None
        kv_hi = [sb(f"kv_hi{i}", [P, KC, TOK], F32R) for i in range(2)]
        kv_lo = [sb(f"kv_lo{i}", [P, KC, TOK], F32R) for i in range(2)]
        q_hi = [sb("q_hi", [P, EC, TOK], F32R)] if rope else kv_hi
        q_lo = [sb("q_lo", [P, EC, TOK], F32R)] if rope else kv_lo
        qk16 = sb("qk16", [P, 2, 2, EC, TOK], F16)
        if rope:
            cs = [sb(f"cs{i}", [P, 2, TOK], F32) for i in range(2)]
            rot = sb("rot", [P, 2, 3, EC, TOK], F32)
        K3 = [sb(f"K3{i}", [ROWS_X, NG, TOK], F16) for i in range(2)]
        Qr = sb("Qr", [SPLIT, NG, TOK], F16)
        head_rows = sb("head_rows", [SPLIT, G], F32)
        Q3 = [sb(f"Q3{i}", [ROWS_X, NG, BPT, G * SEQ], F16) for i in range(2)]
        Vb = [sb(f"Vb{i}", [P, 2, heads, VW], F32) for i in range(2)]
        PT = [sb(f"PT{i}", [P, heads * SEQ], F32) for i in range(2)]
        mx = sb("mx", [P, MCOL], F32)
        mT = sb("mT", [MCOL, P], F16)
        rec = sb("rec", [P, 2, heads // 2, 2], F32)
        On = sb("On", [P, 2, 2, E // 2], F32)
        aT_hi, aT_lo = sb("aT_hi", [P, 2, 2, P], F32R), sb("aT_lo", [P, 2, 2, P], F32R)
        y = sb("y", [P, 2, E], F32)
        stats = sb("stats", [P, 2, 6], F32)
        mv = sb("mv", [P, 2, 2], F32)
        rstd = sb("rstd", [P, 2], F32)
        x_new = [sb(f"xn{i}", [P, 2, E], F32) for i in range(2)]
        bo_bc = sb("bo", [P, E], F32)
        minus_half = sb("mh", [P, 1], F32)
        ident = sb("ident", [P, P], F32)
        if not rope:
            ident_bf = sb("identb", [P, P], BF16)
            mask_q = sb("mask_q", [P, 512], BF16)
            mask_k = sb("mask_k", [P, 512], BF16)
            mask_raw = sb("mask_raw", [P, 2, 512], F32)
            bv_bc = sb("bv", [P, E], F32)
            bqk = sb("bqk", [P, 2, EC], F32)

        psX = [ps(f"psX{i}", [P, 512]) for i in range(2)]
        psM = [ps(f"psM{i}", [P, 512]) for i in range(2)]
        psJ = [ps(f"psJ{i}", [P, 512]) for i in range(2)]
        psO = ps("psO", [P, 2, 512])

        s_const = sem("const_loaded")
        s_in = [sem(f"in_loaded{i}") for i in range(2)]
        s_cs = [sem(f"cos_sin_loaded{i}") for i in range(2)]
        s_tok = [sem(f"tok_loaded{i}") for i in range(2)]
        s_init = sem("buffers_set")
        s_bq = sem("bq_scaled")
        s_mask = sem("masks_cast")
        s_split = sem("inputs_split")
        s_qkproj = sem("qk_projected")
        s_hi = sem("qk_high")
        s_lo = sem("qk_low")
        s_vproj = sem("v_projected")
        s_vb = sem("v_placed")
        s_scr = [sem(f"{n}_parts_stored") for n in "qk"]
        s_qr = sem("q_rows_loaded")
        s_k3 = [sem(f"k_rows_loaded{i}") for i in range(2)]
        s_q3 = sem("q_spread")
        s_mscore = sem("max_scores")
        s_mx = sem("maxima")
        s_mtr = sem("maxima_transposed")
        s_mt = sem("maxima_copied")
        s_mrow = [sem(f"shift_rows{i}") for i in range(2)]
        s_xscore = sem("scores")
        s_exp = sem("probs")
        s_pv = sem("pv_done")
        s_rec = sem("sums_inverted")
        s_on = sem("normalised")
        s_atr = sem("attn_transposed")
        s_ahi = sem("attn_high")
        s_alo = sem("attn_low")
        s_proj = sem("out_projected")
        s_xb = sem("residual_biased")
        s_y = sem("residual_added")
        s_stat = sem("stats_done")
        s_var = sem("variance_done")
        s_eps = sem("eps_added")
        s_rstd = sem("rstd_done")
        s_new = sem("normed")
        s_store = [sem(f"out_stored{i}") for i in range(2)]
        if rope:
            s_xtr = sem("input_transposed")
            s_xhi = sem("input_high")
            s_xlo = sem("input_low")
            s_plain = sem("rot_plain")
            s_swap = sem("rot_swapped")
            s_cos = sem("rot_by_cos")
            s_sin = sem("rot_by_sin")
            s_rot = sem("rotated")
        scratch = consts["scratch"]
        n_in = 2 if rope else 1
        hi_per = 2 if rope else 4
        STEPS = 2 * NX
        i_chunk = [slice(SEQ * b, SEQ * (b + 1)) for b in range(BPT)]

        const_loads = [(bo_bc[:], consts["bo"]), (ident[:], consts["ident"]), (head_rows[:], consts["head_rows"])]
        if not rope:
            const_loads += [(mask_raw[:, 0], consts["mask_q"]), (mask_raw[:, 1], consts["mask_k"]), (bv_bc[:], consts["bv"]), (bqk[:], consts["bqk"])]
        for i in range(2):
            const_loads += [(K3[i][SPLIT:ROWS_X, :, :], consts["k_rows"])]
            if not rope:
                const_loads += [(Q3[i][SPLIT:ROWS_M], consts["q_rows"])]
        def aT_ps():
            return psJ[0][:, 0:2 * P].rearrange("p (b r q) -> p b r q", b=2, r=2)

        def po(pr):
            return psO[:, pr, 0:OW * heads // 2].rearrange("p (h w) -> p h w", w=OW)[:, :, 0:2 * (d_head + 1)].rearrange(
                "p h (b e) -> p h b e", e=d_head + 1)

        block = ctx.enter_context(nc.Block())

        @block.sync
        def _(sp):
            for dst, dram in const_loads:
                sp.dma_start(dst, dram).then_inc(s_const, 16)

            def slot(s):
                e, f, c, d = s.back(-1), s.back(-2), s.back(2), s.back(3)
                i = s.parity
                if there(f):
                    if there(s):
                        sp.wait_ge(s_split, nth(s, 2, 2))
                        if rope:
                            waits_alone(sp)
                            sp.wait_ge(s_xtr, nth(s, 1, 1))
                        waits_alone(sp)
                    if rope:
                        sp.dma_start(kvin[i][:], kv_src[:, :, bass.ds(f.n * TOK, TOK)]).then_inc(s_in[i], 16)
                        sp.dma_start(tok_a[i][:], src["tok"][f.n]).then_inc(s_in[i], 16)
                    else:
                        sp.dma_start(qin[i][:], src["T"][:, :, bass.ds(f.n * TOK, TOK)]).then_inc(s_in[i], 16)
                if rope and there(e):
                    if there(s.back(1)):
                        sp.wait_ge(s_cos, nth(s.back(1), 2, 2))
                        waits_alone(sp)
                        sp.wait_ge(s_sin, nth(s.back(1), 2, 2))
                        waits_alone(sp)
                    sp.dma_start(cs[1 - i][:], consts["cs"][:, :, bass.ds(e.n * TOK, TOK)]).then_inc(s_cs[1 - i], 16)
                if there(c):
                    if there(c.back(2)):
                        sp.wait_ge(s_y, nth(c.back(2), 2, 2))
                        waits_alone(sp)
                    sp.dma_start(tok_in[i][:], src["tok"][c.n]).then_inc(s_tok[i], 16)
                if there(s):
                    if there(c):
                        sp.wait_ge(s_k3[i], dmas(c, 3))
                        waits_alone(sp)
                    for o in range(2):
                        sp.wait_ge(s_hi, nth(s, hi_per, hi_per // 2 * (o + 1)))
                        sp.wait_ge(s_lo, nth(s, hi_per, hi_per // 2 * (o + 1)))
                        sp.dma_start(scratch[i, o].rearrange("r g a n -> g r (a n)"),
                                     qk16[:, o].rearrange("p a c n -> p (a c n)")).then_inc(s_scr[o], 16)
                        sp.wait_ge(s_scr[o], (s.n + 1) * 16)
                        if there(c):
                            if o:
                                sp.wait_ge(s_xscore, nth(c, STEPS, STEPS))
                            else:
                                sp.wait_ge(s_q3, nth(s.back(1), G, G))
                        for k, part in enumerate(((0, 1, 0), (0, 0, 1))[o]):
                            to = (Qr, K3[i])[o][bass.ts(k, E // NG)].rearrange("r g n -> r (g n)")
                            sp.dma_start(to, scratch[i, o, :, :, part]).then_inc((s_qr, s_k3[i])[o], 16)
                if there(d):
                    sp.wait_ge(s_new, nth(d, 2, 2))
                    waits_alone(sp)
                    sp.dma_start(x_out[d.n], x_new[1 - i][:]).then_inc(s_store[1 - i], 16)

            run_slots(sp, slot, 4, NT + 2, first=-2)
            for i in range(2):
                sp.wait_ge(s_store[i], 16 * NT // 2)

        @block.gpsimd
        def _(pool):
            nc.gpsimd.memset(minus_half[:], -0.5).then_inc(s_init, 1)
            for i in range(2):
                nc.gpsimd.memset(Vb[i][:], 0.0).then_inc(s_init, 1)
            pool.wait_ge(s_init, 3)
            if not rope:
                pool.wait_ge(s_const, 16 * len(const_loads))
                nc.gpsimd.tensor_scalar(bqk[:, 0], bqk[:, 0], d_head ** -0.5, None, ALU.mult).then_inc(s_bq, 1)
                pool.wait_ge(s_bq, 1)
            for i in range(2):
                for b in range(2):
                    col = b * (d_head + 1) + d_head
                    nc.gpsimd.memset(Vb[i][b * SEQ:(b + 1) * SEQ, :, :, col:col + 1], 1.0).then_inc(s_init, 1)
                    pool.wait_ge(s_init, 4 + 2 * i + b)
            pool.wait_ge(s_const, 16 * len(const_loads))

            def by_cos(s, o):
                pool.wait_ge(s_plain, nth(s, 2, o + 1))
                if o == 0:
                    pool.wait_ge(s_cs[s.parity], dmas(s, 1))
                if there(s.back(1)):
                    pool.wait_ge(s_rot, nth(s.back(1), 2, o + 1))
                nc.gpsimd.tensor_tensor(rot[:, o, 2], rot[:, o, 0],
                                        cs[s.parity][:, 0:1, :].to_broadcast([P, EC, TOK]), ALU.mult).then_inc(s_cos, 1)

            def low_parts(s, o):
                pool.wait_ge(s_rot, nth(s, 2, o + 1))
                pool.wait_ge(s_hi, nth(s, 2, o + 1))
                if there(s.back(1)):
                    pool.wait_ge(s_scr[o], s.n * 16)
                nc.gpsimd.tensor_tensor(qk16[:, o, 1], rot[:, o, 1], qk16[:, o, 0], ALU.subtract).then_inc(s_lo, 1)

            def split_input(s):
                i = s.parity
                pool.wait_ge(s_in[i], dmas(s, n_in))
                if there(s.back(2)):
                    pool.wait_ge(s_vproj, nth(s.back(2), 1, 1))
                waits_alone(pool)
                raw = kvin[i] if rope else qin[i]
                nc.gpsimd.tensor_copy(kv_hi[i][:], raw[:]).then_inc(s_split, 1)
                pool.wait_ge(s_split, nth(s, 2, 1))
                nc.gpsimd.tensor_tensor(kv_lo[i][:], raw[:], kv_hi[i][:].bitcast(F32), ALU.subtract).then_inc(s_split, 1)

            def add_out_bias(c):
                i = c.parity
                pool.wait_ge(s_tok[i], dmas(c, 1))
                nc.gpsimd.tensor_tensor(tok_in[i][:], tok_in[i][:],
                                        bo_bc[:].rearrange("p (o n) -> p o n", o=1).to_broadcast([P, 2, E]),
                                        ALU.add).then_inc(s_xb, 1)

            def layer_norm(c, pr):
                pool.wait_ge(s_var, nth(c, 2, pr + 1))
                waits_alone(pool)
                nc.gpsimd.tensor_scalar(rstd[:, pr:pr + 1], mv[:, pr, 1:2], LN_EPS, None, ALU.add).then_inc(s_eps, 1)
                pool.wait_ge(s_eps, nth(c, 2, pr + 1))
                nc.gpsimd.tensor_tensor(rstd[:, pr:pr + 1], rstd[:, pr:pr + 1], minus_half[:],
                                        ALU.pow).then_inc(s_rstd, 1)
                pool.wait_ge(s_rstd, nth(c, 2, pr + 1))
                if pr == 0 and there(c.back(2)):
                    pool.wait_ge(s_store[c.parity], dmas(c.back(2), 1))
                waits_alone(pool)
                nc.gpsimd.tensor_scalar(x_new[c.parity][:, pr], y[:, pr], mv[:, pr, 0:1], rstd[:, pr:pr + 1],
                                        ALU.subtract, ALU.mult).then_inc(s_new, 1)

            def slot(s):
                e, c, d = s.back(-1), s.back(2), s.back(3)
                if rope and there(s):
                    by_cos(s, 0)
                    by_cos(s, 1)
                    low_parts(s, 0)
                if there(c):
                    add_out_bias(c)
                if there(d):
                    layer_norm(d, 1)
                if rope and there(s):
                    low_parts(s, 1)
                if there(e):
                    split_input(e)
                if there(c):
                    layer_norm(c, 0)

            run_slots(pool, slot, 6, NT + 2, first=-1)

        @block.scalar
        def _(act):
            act.wait_ge(s_const, 16 * len(const_loads))
            if not rope:
                act.wait_ge(s_bq, 1)

            def high_parts(s, o):
                if there(s.back(1)):
                    act.wait_ge(s_scr[o], (s.n) * 16)
                if rope:
                    act.wait_ge(s_rot, nth(s, 2, o + 1))
                    nc.scalar.activation(qk16[:, o, 0], rot[:, o, 1], ACT.Copy).then_inc(s_hi, 1)
                    return
                act.wait_ge(s_qkproj, nth(s, 2, o + 1))
                for ch in range(EC):
                    nc.scalar.activation(qk16[:, o, 0, ch], psJ[o][:, bass.ts(ch, TOK)], ACT.Identity,
                                         bias=bqk[:, o, ch:ch + 1]).then_inc(s_hi, 1)

            def plain(s, o):
                act.wait_ge(s_qkproj, nth(s, 2, o + 1))
                if there(s.back(1)):
                    act.wait_ge(s_swap, nth(s.back(1), 2, o + 1))
                    act.wait_ge(s_cos, nth(s.back(1), 2, o + 1))
                nc.scalar.activation(rot[:, o, 0], psJ[o][:].rearrange("p (c n) -> p c n", c=EC), ACT.Copy,
                                     scale=1.0 if o else d_head ** -0.5).then_inc(s_plain, 1)

            def probs(c, k):
                pr, x = divmod(k, NX)
                act.wait_ge(s_xscore, nth(c, STEPS, k + 1))
                if there(c.back(1)):
                    act.wait_ge(s_pv, nth(c.back(1), 2, pr + 1))
                nc.scalar.activation(PT[pr][:, bass.ts(x, 512)], psX[k % 2][:], ACT.Exp).then_inc(s_exp, 1)

            def attn_high(c, pr):
                act.wait_ge(s_atr, nth(c, 2, pr + 1))
                if there(c.back(1)):
                    act.wait_ge(s_proj, nth(c.back(1), 2, pr + 1))
                nc.scalar.activation(aT_hi[:, pr].rearrange("p r (b q) -> p b r q", b=2), aT_ps(),
                                     ACT.Copy).then_inc(s_ahi, 1)

            def input_high(e):
                act.wait_ge(s_xtr, nth(e, 1, 1))
                if there(e.back(1)):
                    act.wait_ge(s_qkproj, nth(e.back(1), 2, 1))
                nc.scalar.activation(q_hi[0][:], psJ[1][:].rearrange("p (c n) -> p c n", c=EC),
                                     ACT.Copy).then_inc(s_xhi, 1)

            def place_v(s):
                act.wait_ge(s_vproj, nth(s, 1, 1))
                for b in range(2):
                    rows = slice(b * SEQ, (b + 1) * SEQ)
                    nc.scalar.activation(Vb[s.parity][rows, :, :, b * (d_head + 1):b * (d_head + 1) + d_head],
                                         psJ[1][rows, :].rearrange("p (r h e) -> p r h e", r=2, e=d_head),
                                         ACT.Copy).then_inc(s_vb, 1)

            def slot(s):
                e, b_, c, d = s.back(-1), s.back(1), s.back(2), s.back(3)
                if there(s):
                    plain(s, 0) if rope else high_parts(s, 0)
                for k in range(NX):
                    if there(c):
                        probs(c, k)
                    if k == 0 and there(s):
                        plain(s, 1) if rope else high_parts(s, 1)
                    if k == 1 and there(s) and rope:
                        high_parts(s, 0)
                    if k == NX - 2 and there(d):
                        attn_high(d, 1)
                if rope and there(b_):
                    place_v(b_)
                if rope and there(s):
                    high_parts(s, 1)
                for k in range(NX, STEPS):
                    if there(c):
                        probs(c, k)
                        if k == NX + NX // 2 - 1:
                            attn_high(c, 0)
                if rope and there(e):
                    input_high(e)
                if there(b_):
                    act.wait_ge(s_mt, nth(b_, 1, 1))
                    act.dma_start(Q3[b_.parity][ROWS_M:ROWS_X], mT[:]).then_inc(s_mrow[b_.parity], 16)

            run_slots(act, slot, 4, NT + 2, first=-1)

        @block.vector
        def _(dve):
            dve.wait_ge(s_const, 16 * len(const_loads))
            dve.wait_ge(s_init, 7)

            if not rope:
                nc.vector.tensor_copy(mask_q[:], mask_raw[:, 0]).then_inc(s_mask, 1)
                nc.vector.tensor_copy(mask_k[:], mask_raw[:, 1]).then_inc(s_mask, 1)
                nc.vector.tensor_copy(ident_bf[:], ident[:]).then_inc(s_mask, 1)

            def spread_q(s):
                i = s.parity
                dve.wait_ge(s_qr, nth(s, 48, 48))
                if there(s.back(2)):
                    dve.wait_ge(s_xscore, nth(s.back(2), STEPS, STEPS))
                for h in range(G):
                    nc.vector.tensor_scalar(Q3[i][0:SPLIT, :, :, bass.ts(h, SEQ)].rearrange("r g b q -> r (g b) q"),
                                            Qr[:].rearrange("r g (b q) -> r (g b) q", q=SEQ), head_rows[:, h:h + 1],
                                            None, ALU.mult).then_inc(s_q3, 1)

            def low_parts(s, o):
                dve.wait_ge(s_hi, nth(s, 4, 2 * o + 2))
                for ch in range(EC):
                    nc.vector.scalar_tensor_tensor(qk16[:, o, 1, ch], psJ[o][:, bass.ts(ch, TOK)],
                                                   bqk[:, o, ch:ch + 1], qk16[:, o, 0, ch],
                                                   ALU.add, ALU.subtract).then_inc(s_lo, 1)

            def swapped_by_sin(s, o):
                dve.wait_ge(s_plain, nth(s, 2, o + 1))
                if there(s.back(1)):
                    dve.wait_ge(s_lo, nth(s.back(1), 2, o + 1))
                    dve.wait_ge(s_hi, nth(s.back(1), 2, o + 1))
                waits_alone(dve)
                nc.vector.stream_shuffle(rot[:, o, 1], rot[:, o, 0], [n ^ 1 for n in range(32)]).then_inc(s_swap, 1)
                dve.wait_ge(s_swap, nth(s, 2, o + 1))
                if o == 0:
                    dve.wait_ge(s_cs[s.parity], dmas(s, 1))
                nc.vector.tensor_tensor(rot[:, o, 1], rot[:, o, 1],
                                        cs[s.parity][:, 1:2, :].to_broadcast([P, EC, TOK]), ALU.mult).then_inc(s_sin, 1)

            def rotated(s, o):
                dve.wait_ge(s_sin, nth(s, 2, o + 1))
                dve.wait_ge(s_cos, nth(s, 2, o + 1))
                nc.vector.tensor_tensor(rot[:, o, 1], rot[:, o, 1], rot[:, o, 2], ALU.add).then_inc(s_rot, 1)

            def maxima(b_, m):
                dve.wait_ge(s_mscore, nth(b_, STEPS, m + 1))
                if m == 0 and there(b_.back(1)):
                    dve.wait_ge(s_mtr, nth(b_.back(1), 1, 1))
                nc.vector.tensor_reduce(mx[:, bass.ts(m, 8)], psM[m % 2][:].rearrange("p (c k) -> p c k", k=SEQ),
                                        AX_X, ALU.max).then_inc(s_mx, 1)

            def normalise(c, pr):
                dve.wait_ge(s_pv, nth(c, 2, pr + 1))
                o = po(pr)
                nc.vector.reciprocal(rec[:, pr], o[:, :, :, d_head:d_head + 1].rearrange("p h b e -> p h (b e)"))\
                    .then_inc(s_rec, 1)
                dve.wait_ge(s_rec, nth(c, 2, pr + 1))
                if there(c.back(1)):
                    dve.wait_ge(s_atr, nth(c.back(1), 2, pr + 1))
                nc.vector.tensor_tensor(
                    On[:, pr].rearrange("p b (h e) -> p b h e", e=d_head),
                    o[:, :, :, 0:d_head].rearrange("p h b e -> p b h e"),
                    rec[:, pr].rearrange("p h (b e) -> p b h e", e=1).to_broadcast([P, 2, heads // 2, d_head]),
                    ALU.mult).then_inc(s_on, 1)

            def attn_low(c, pr):
                dve.wait_ge(s_ahi, nth(c, 2, pr + 1))
                nc.vector.tensor_tensor(aT_lo[:, pr].rearrange("p r (b q) -> p b r q", b=2), aT_ps(),
                                        aT_hi[:, pr].bitcast(F32).rearrange("p r (b q) -> p b r q", b=2),
                                        ALU.subtract).then_inc(s_alo, 1)

            def place_v(s):
                dve.wait_ge(s_vproj, nth(s, 1, 1))
                for b in range(2):
                    rows = slice(b * SEQ, (b + 1) * SEQ)
                    out = Vb[s.parity][rows, :, :, b * (d_head + 1):b * (d_head + 1) + d_head]
                    v = psJ[1][rows, :].rearrange("p (r h e) -> p r h e", r=2, e=d_head)
                    bias = bv_bc[rows, :].rearrange("p (r h e) -> p r h e", r=1, e=d_head)
                    nc.vector.tensor_tensor(out, v, bias.to_broadcast([SEQ, 2, heads, d_head]),
                                            ALU.add).then_inc(s_vb, 1)

            def residual(c, pr):
                dve.wait_ge(s_proj, nth(c, 2, pr + 1))
                dve.wait_ge(s_xb, nth(c, 1, 1))
                if there(c.back(1)):
                    dve.wait_ge(s_new, nth(c.back(1), 2, pr + 1))
                nc.vector.tensor_tensor(y[:, pr], psJ[0][:, 0:E], tok_in[c.parity][:, pr], ALU.add).then_inc(s_y, 1)
                dve.wait_ge(s_y, nth(c, 2, pr + 1))
                nc.vector.bn_stats(stats[:, pr], y[:, pr]).then_inc(s_stat, 1)
                dve.wait_ge(s_stat, nth(c, 2, pr + 1))
                waits_alone(dve)
                nc.vector.bn_aggr(mv[:, pr], stats[:, pr]).then_inc(s_var, 1)

            def input_low(e):
                dve.wait_ge(s_xhi, nth(e, 1, 1))
                nc.vector.tensor_tensor(q_lo[0][:], psJ[1][:].rearrange("p (c n) -> p c n", c=EC),
                                        q_hi[0][:].bitcast(F32), ALU.subtract).then_inc(s_xlo, 1)

            def shifts(b_):
                dve.wait_ge(s_mtr, nth(b_, 1, 1))
                if there(b_.back(1)):
                    dve.wait_ge(s_mrow[1 - b_.parity], dmas(b_.back(1), 1))
                nc.vector.tensor_scalar(mT[:], psJ[0][0:MCOL, 0:P], M_CLAMP, -M_CLAMP,
                                        ALU.min, ALU.max).then_inc(s_mt, 1)

            def slot(s):
                e, b_, c, d = s.back(-1), s.back(1), s.back(2), s.back(3)
                if there(s) and not rope:
                    low_parts(s, 0)
                for k in range(NX):
                    if k == 1 and there(s):
                        rotated(s, 0) if rope else low_parts(s, 1)
                    if k == NX - 1 and there(d):
                        attn_low(d, 1)
                    if there(b_):
                        maxima(b_, k)
                    if k == 0 and there(s) and rope:
                        swapped_by_sin(s, 0)
                if there(d):
                    residual(d, 1)
                if rope and there(s):
                    swapped_by_sin(s, 1)
                    rotated(s, 1)
                if not rope and there(b_):
                    place_v(b_)
                if there(c):
                    normalise(c, 0)
                for k in range(NX, STEPS):
                    if there(b_):
                        maxima(b_, k)
                    if k == NX + NX // 2 - 1 and there(c):
                        attn_low(c, 0)
                if there(c):
                    residual(c, 0)
                if there(b_):
                    shifts(b_)
                if rope and there(e):
                    input_low(e)
                if there(s):
                    spread_q(s)
                if there(c):
                    normalise(c, 1)

            run_slots(dve, slot, 4, NT + 2, first=-1)

        @block.tensor
        def _(pe):
            pe.wait_ge(s_const, 16 * len(const_loads))
            pe.wait_ge(s_init, 7)
            if not rope:
                pe.wait_ge(s_mask, 3)

            def qk_copied(s, o):
                if rope:
                    pe.wait_ge(s_plain, nth(s, 2, o + 1))
                else:
                    pe.wait_ge(s_lo, nth(s, 4, 2 * o + 2))

            def project(s, o):
                w, hi, lo = (wk, kv_hi, kv_lo) if o else (wq, q_hi, q_lo)
                x_hi, x_lo = (hi[s.parity], lo[s.parity]) if o or not rope else (hi[0], lo[0])
                n_k = KC if o else EC
                for ch in range(EC):
                    for k in range(n_k):
                        last = mm3(nc, psJ[o][:, bass.ts(ch, TOK)], w[0][:, k, bass.ts(ch, P)],
                                   w[1][:, k, bass.ts(ch, P)], x_hi[:, k], x_lo[:, k], k == 0, k == n_k - 1)
                last.then_inc(s_qkproj, 1)

            def max_scores(b_, m):
                if m or there(b_.back(1)):
                    if not (m == 1 and not there(b_.back(1))):
                        pe.wait_ge(s_mx, nth(b_, STEPS, m - 1))
                if m == 0:
                    pe.wait_ge(s_q3, nth(b_, G, G))
                    pe.wait_ge(s_k3[b_.parity], dmas(b_, 3))
                out, i = psM[m % 2], b_.parity
                if not rope:
                    nc.tensor.matmul(out[:], ident_bf[:], mask_q[:], start=True, stop=True, skip_group_check=True)
                for k in range(8):
                    g, b, a = (m * 8 + k) // (BPT * G // 2), (m * 8 + k) // (G // 2) % BPT, k % (G // 2)
                    last = nc.tensor.matmul(out[:, bass.ts(k, SEQ)], Q3[i][0:ROWS_M, g, b, bass.ts(a, P)],
                                            K3[i][0:ROWS_M, g, i_chunk[b]], start=rope and k == 0, stop=True,
                                            skip_group_check=True)
                last.then_inc(s_mscore, 1)

            def scores(c, k):
                pr, x = divmod(k, NX)
                i, out = c.parity, psX[k % 2]
                if k > 1 or there(c.back(1)):
                    pe.wait_ge(s_exp, nth(c, STEPS, k - 1))
                if k == 0:
                    pe.wait_ge(s_mrow[i], dmas(c, 1))
                if not rope:
                    nc.tensor.matmul(out[:], ident_bf[:], mask_k[:], start=True, stop=True, skip_group_check=True)
                n_g = 8 // G
                for b in range(2):
                    for n in range(n_g):
                        g, b4 = x * n_g + n, 2 * pr + b
                        last = nc.tensor.matmul(out[b * SEQ:(b + 1) * SEQ, bass.ts(n, G * SEQ)],
                                                K3[i][0:ROWS_X, g, i_chunk[b4]], Q3[i][0:ROWS_X, g, b4],
                                                start=rope and n == 0, stop=True, skip_group_check=True)
                last.then_inc(s_xscore, 1)

            def attend(c, pr):
                if there(c.back(1)):
                    pe.wait_ge(s_on, nth(c.back(1), 2, pr + 1))
                pe.wait_ge(s_vb, nth(c, 2, 2))
                for h in range(heads):
                    if h % 8 == 0:
                        pe.wait_ge(s_exp, nth(c, STEPS, pr * NX + h // 8 + 1))
                    col = h // 2 * OW
                    last = nc.tensor.matmul(psO[(h % 2) * SEQ:(h % 2 + 1) * SEQ, pr, col:col + VW],
                                            PT[pr][:, bass.ts(h, SEQ)], Vb[c.parity][:, pr, h, :],
                                            start=True, stop=True, skip_group_check=True)
                last.then_inc(s_pv, 1)

            def transpose_attn(c, pr):
                pe.wait_ge(s_on, nth(c, 2, pr + 1))
                for b in range(2):
                    last = nc.tensor.transpose(psJ[0][:, bass.ts(b, P)], On[:, pr, b], ident[:])
                last.then_inc(s_atr, 1)

            def project_out(c, pr):
                pe.wait_ge(s_alo, nth(c, 2, pr + 1))
                for r in range(2):
                    last = mm3(nc, psJ[0][:, 0:E], aT_hi[:, pr, r], aT_lo[:, pr, r], wo[0][:, r], wo[1][:, r],
                               r == 0, r == 1)
                last.then_inc(s_proj, 1)

            def transpose_input(e):
                pe.wait_ge(s_in[e.parity], dmas(e, n_in))
                if there(e.back(2)):
                    pe.wait_ge(s_vb, nth(e.back(2), 2, 2))
                elif there(e.back(1)):
                    qk_copied(e.back(1), 1)
                for r in range(2):
                    for ch in range(EC):
                        last = nc.tensor.transpose(psJ[1][:, ch * TOK + r * P:ch * TOK + (r + 1) * P],
                                                   tok_a[e.parity][:, r, bass.ts(ch, P)], ident[:])
                last.then_inc(s_xtr, 1)

            def project_v(s):
                for pr in range(2):
                    for k in range(KC):
                        x = bass.ts(pr, P)
                        last = mm3(nc, psJ[1][:, bass.ts(pr, E)], kv_hi[s.parity][:, k, x], kv_lo[s.parity][:, k, x],
                                   wv[0][:, k], wv[1][:, k], k == 0, k == KC - 1)
                last.then_inc(s_vproj, 1)

            def transpose_maxima(b_):
                pe.wait_ge(s_mx, nth(b_, STEPS, STEPS))
                waits_alone(pe)
                nc.tensor.transpose(psJ[0][0:MCOL, 0:P], mx[:], ident[:]).then_inc(s_mtr, 1)

            def slot(s):
                e, b_, c, d = s.back(-1), s.back(1), s.back(2), s.back(3)
                if there(s):
                    if rope:
                        pe.wait_ge(s_xlo, nth(s, 1, 1))
                    else:
                        pe.wait_ge(s_split, nth(s, 2, 2))
                    if there(c):
                        pe.wait_ge(s_mt, nth(c, 1, 1))
                    elif there(b_):
                        qk_copied(b_, 0)
                    project(s, 0)
                for k in range(NX):
                    if k == 1 and there(s):
                        if rope:
                            pe.wait_ge(s_split, nth(s, 2, 2))
                        elif there(c):
                            pe.wait_ge(s_vb, nth(c, 2, 2))
                        elif there(b_):
                            qk_copied(b_, 1)
                        project(s, 1)
                    if k == NX - 1 and there(d):
                        if there(s):
                            qk_copied(s, 0)
                        elif there(c):
                            pe.wait_ge(s_mt, nth(c, 1, 1))
                        else:
                            pe.wait_ge(s_y, nth(d, 2, 1))
                        transpose_attn(d, 1)
                    if there(c):
                        scores(c, k)
                    if there(b_):
                        max_scores(b_, k)
                if there(d):
                    project_out(d, 1)
                if there(b_):
                    if there(s):
                        qk_copied(s, 1)
                    elif there(c):
                        pe.wait_ge(s_vb, nth(c, 2, 2))
                    project_v(b_)
                if there(c):
                    attend(c, 0)
                for k in range(NX, STEPS):
                    if k == NX + NX // 2 and there(c):
                        if there(d):
                            pe.wait_ge(s_y, nth(d, 2, 2))
                        elif there(s):
                            qk_copied(s, 0)
                        transpose_attn(c, 0)
                    if there(c):
                        scores(c, k)
                    if there(b_):
                        max_scores(b_, k)
                if there(c):
                    project_out(c, 0)
                if rope and there(e):
                    transpose_input(e)
                if there(b_):
                    if there(c):
                        pe.wait_ge(s_y, nth(c, 2, 1))
                    elif there(s):
                        qk_copied(s, 0)
                    transpose_maxima(b_)
                if there(c):
                    attend(c, 1)

            run_slots(pe, slot, 4, NT + 2, first=-1)


def ffn(nc, x_in, w_dram, out, consts):
    FT = 4
    N = FT * P
    NTF = NSEQ * SEQ // N
    HC = HID // P

    with ExitStack() as ctx:
        def sb(name, shape, dt):
            return ctx.enter_context(nc.sbuf_tensor(f"f_{name}", shape, dt))

        def ps(name, shape):
            return ctx.enter_context(nc.psum_tensor(f"f_{name}", shape, F32))

        def sem(name):
            return ctx.enter_context(nc.semaphore(f"f_{name}"))

        wg = [sb(f"wg{i}", [P, EC, HID], F32R) for i in range(2)]
        wu = [sb(f"wu{i}", [P, EC, HID], F32R) for i in range(2)]
        wd = [sb(f"wd{i}", [P, HC, E], F32R) for i in range(2)]
        with ExitStack() as raw_ctx:
            raws = [raw_ctx.enter_context(nc.sbuf_tensor(f"f_raw{i}", shape, F32))
                    for i, shape in enumerate(([P, EC, HID], [P, EC, HID], [P, HC, E]))]
            split_weights(nc, [(w_dram[n], r[:], w[0][:], w[1][:], 1.0)
                               for n, r, w in zip(("wg", "wu", "wd"), raws, (wg, wu, wd))])

        x_tok = [sb(f"x_tok{i}", [P, FT, E], F32) for i in range(2)]
        x_res = [sb(f"x_res{i}", [P, FT, E], F32) for i in range(2)]
        x_hi, x_lo = sb("x_hi", [P, EC, N], F32R), sb("x_lo", [P, EC, N], F32R)
        gate = [sb(f"gate{i}", [P, N], F32) for i in range(2)]
        hid = [sb(f"hid{i}", [P, N], F32) for i in range(2)]
        h_hi = [sb(f"h_hi{i}", [P, HC, N], F32R) for i in range(2)]
        h_lo = [sb(f"h_lo{i}", [P, HC, N], F32R) for i in range(2)]
        y = sb("y", [P, FT, E], F32)
        stats = sb("stats", [P, FT, 6], F32)
        mv = sb("mv", [P, FT, 2], F32)
        rstd = sb("rstd", [P, FT], F32)
        x_new = [sb(f"xn{i}", [P, FT, E], F32) for i in range(2)]
        minus_half = sb("mh", [P, FT], F32)
        ident = sb("ident", [P, P], F32)

        psT = [ps(f"psT{i}", [P, N]) for i in range(2)]
        psG = [ps(f"psG{i}", [P, N]) for i in range(2)]
        psU = [ps(f"psU{i}", [P, N]) for i in range(2)]
        psD = [ps(f"psD{i}", [P, 2, E]) for i in range(2)]

        s_const = sem("const_loaded")
        s_init = sem("constants_set")
        s_in = [sem(f"in_loaded{i}") for i in range(2)]
        s_res = [sem(f"res_loaded{i}") for i in range(2)]
        s_xtr = sem("input_transposed")
        s_xhi = sem("input_high")
        s_xlo = sem("input_low")
        s_gate = sem("gate_done")
        s_up = sem("up_done")
        s_silu = sem("silu_done")
        s_h = sem("hidden_done")
        s_hhi = sem("hidden_high")
        s_hlo = sem("hidden_low")
        s_down = sem("down_done")
        s_y = sem("residual_added")
        s_stat = sem("stats_done")
        s_var = sem("variance_done")
        s_eps = sem("eps_added")
        s_rstd = sem("rstd_done")
        s_new = sem("normed")
        s_store = [sem(f"out_stored{i}") for i in range(2)]
        block = ctx.enter_context(nc.Block())

        def is_tile(t):
            return there(t, NTF)

        @block.sync
        def _(sp):
            sp.dma_start(ident[:], consts["ident"]).then_inc(s_const, 16)

            def slot(u):
                v, c, i = u.back(1), u.back(2), u.parity
                if is_tile(u):
                    if is_tile(c):
                        sp.wait_ge(s_xtr, nth(c, 1, 1))
                        waits_alone(sp)
                    sp.dma_start(x_tok[i][:].rearrange("p (a r) e -> p a r e", a=2), x_in[u.n])\
                        .then_inc(s_in[i], 16)
                if is_tile(v):
                    if is_tile(v.back(2)):
                        sp.wait_ge(s_y, nth(v.back(2), 2, 2))
                        waits_alone(sp)
                    sp.dma_start(x_res[1 - i][:].rearrange("p (a r) e -> p a r e", a=2), x_in[v.n])\
                        .then_inc(s_res[1 - i], 16)
                if is_tile(c):
                    sp.wait_ge(s_new, nth(c, FT, FT))
                    waits_alone(sp)
                    sp.dma_start(out[c.n], x_new[i][:]).then_inc(s_store[i], 16)

            run_slots(sp, slot, 4, NTF + 1, NTF)
            for i in range(2):
                sp.wait_ge(s_store[i], 16 * NTF // 2)

        @block.scalar
        def _(act):
            def slot(s):
                if not is_tile(s):
                    return
                for ch in range(EC):
                    act.wait_ge(s_xtr, nth(s, 1, 1))
                    if is_tile(s.back(1)):
                        act.wait_ge(s_up, nth(s.back(1), HC, HC))
                    nc.scalar.activation(x_hi[:, ch], psT[ch][:], ACT.Copy).then_inc(s_xhi, 1)
                for h in range(HC):
                    b = h % 2
                    act.wait_ge(s_gate, nth(s, HC, h + 1))
                    if h > 1 or is_tile(s.back(1)):
                        act.wait_ge(s_h, nth(s, HC, h - 1))
                    nc.scalar.activation(gate[b][:], psG[b][:], ACT.Silu).then_inc(s_silu, 1)
                    act.wait_ge(s_h, nth(s, HC, h + 1))
                    if is_tile(s.back(2)):
                        act.wait_ge(s_down, nth(s.back(2), FT, FT))
                    nc.scalar.activation(h_hi[s.parity][:, h], hid[b][:], ACT.Copy).then_inc(s_hhi, 1)

            run_slots(act, slot, 4, NTF - 1, NTF)

        @block.vector
        def _(dve):
            def slot(s):
                c = s.back(1)
                if is_tile(s):
                    for ch in range(EC):
                        dve.wait_ge(s_xhi, nth(s, EC, ch + 1))
                        nc.vector.tensor_tensor(x_lo[:, ch], psT[ch][:], x_hi[:, ch].bitcast(F32),
                                                ALU.subtract).then_inc(s_xlo, 1)
                for h in range(HC):
                    b = h % 2
                    if is_tile(s):
                        dve.wait_ge(s_silu, nth(s, HC, h + 1))
                        dve.wait_ge(s_up, nth(s, HC, h + 1))
                        if h > 1 or is_tile(s.back(1)):
                            dve.wait_ge(s_hlo, nth(s, HC, h - 1))
                        nc.vector.tensor_tensor(hid[b][:], gate[b][:], psU[b][:], ALU.mult).then_inc(s_h, 1)
                    if is_tile(c) and h in (4, 7):
                        half = h // 7
                        dve.wait_ge(s_down, nth(c, FT, 2 * half + 2))
                        dve.wait_ge(s_res[c.parity], dmas(c, 1))
                        if is_tile(c.back(1)):
                            dve.wait_ge(s_new, nth(c.back(1), FT, 2 * half + 2))
                        nc.vector.tensor_tensor(y[:, 2 * half:2 * half + 2], psD[half][:],
                                                x_res[c.parity][:, 2 * half:2 * half + 2], ALU.add).then_inc(s_y, 1)
                        dve.wait_ge(s_y, nth(c, 2, half + 1))
                        for r in range(2 * half, 2 * half + 2):
                            nc.vector.bn_stats(stats[:, r], y[:, r]).then_inc(s_stat, 1)
                        dve.wait_ge(s_stat, nth(c, FT, 2 * half + 2))
                        waits_alone(dve)
                        for r in range(2 * half, 2 * half + 2):
                            nc.vector.bn_aggr(mv[:, r], stats[:, r]).then_inc(s_var, 1)

            run_slots(dve, slot, 4, NTF, NTF)

        @block.gpsimd
        def _(pool):
            nc.gpsimd.memset(minus_half[:], -0.5).then_inc(s_init, 1)
            pool.wait_ge(s_init, 1)

            def slot(s):
                c = s.back(1)
                for h in range(HC):
                    if is_tile(s):
                        pool.wait_ge(s_hhi, nth(s, HC, h + 1))
                        nc.gpsimd.tensor_tensor(h_lo[s.parity][:, h], hid[h % 2][:],
                                                h_hi[s.parity][:, h].bitcast(F32), ALU.subtract).then_inc(s_hlo, 1)
                    if is_tile(c) and h in (5, 7):
                        half = h // 7
                        rows = slice(2 * half, 2 * half + 2)
                        pool.wait_ge(s_var, nth(c, FT, 2 * half + 2))
                        waits_alone(pool)
                        nc.gpsimd.tensor_scalar(rstd[:, rows], mv[:, rows, 1:2].rearrange("p r e -> p (r e)"), LN_EPS,
                                                None, ALU.add).then_inc(s_eps, 1)
                        pool.wait_ge(s_eps, nth(c, 2, half + 1))
                        nc.gpsimd.tensor_tensor(rstd[:, rows], rstd[:, rows], minus_half[:, rows],
                                                ALU.pow).then_inc(s_rstd, 1)
                        pool.wait_ge(s_rstd, nth(c, 2, half + 1))
                        if half == 0 and is_tile(c.back(2)):
                            pool.wait_ge(s_store[c.parity], dmas(c.back(2), 1))
                        waits_alone(pool)
                        for r in range(2 * half, 2 * half + 2):
                            nc.gpsimd.tensor_scalar(x_new[c.parity][:, r], y[:, r], mv[:, r, 0:1], rstd[:, r:r + 1],
                                                    ALU.subtract, ALU.mult).then_inc(s_new, 1)

            run_slots(pool, slot, 4, NTF, NTF)

        @block.tensor
        def _(pe):
            pe.wait_ge(s_const, 16)

            def slot(s):
                c = s.back(1)
                if is_tile(s):
                    pe.wait_ge(s_in[s.parity], dmas(s, 1))
                    if is_tile(c):
                        pe.wait_ge(s_xlo, nth(c, EC, EC))
                    for ch in range(EC):
                        for r in range(FT):
                            last = nc.tensor.transpose(psT[ch][:, bass.ts(r, P)], x_tok[s.parity][:, r, bass.ts(ch, P)],
                                                       ident[:])
                    last.then_inc(s_xtr, 1)
                    pe.wait_ge(s_xlo, nth(s, EC, EC))
                for h in range(HC):
                    if is_tile(s):
                        if h > 1 or is_tile(c):
                            pe.wait_ge(s_silu, nth(s, HC, h - 1))
                            pe.wait_ge(s_h, nth(s, HC, h - 1))
                        for w, bank, done in ((wg, psG[h % 2], s_gate), (wu, psU[h % 2], s_up)):
                            for k in range(EC):
                                last = mm3(nc, bank[:], w[0][:, k, bass.ts(h, P)], w[1][:, k, bass.ts(h, P)],
                                           x_hi[:, k], x_lo[:, k], k == 0, k == EC - 1)
                            last.then_inc(done, 1)
                    if is_tile(c) and h % 2:
                        r = h // 2
                        if r == 0:
                            pe.wait_ge(s_hlo, nth(c, HC, HC))
                        if is_tile(c.back(1)):
                            pe.wait_ge(s_y, nth(c.back(1), 2, r // 2 + 1))
                        for k in range(HC):
                            x = bass.ts(r, P)
                            last = mm3(nc, psD[r // 2][:, r % 2], h_hi[c.parity][:, k, x], h_lo[c.parity][:, k, x],
                                       wd[0][:, k], wd[1][:, k], k == 0, k == HC - 1)
                        last.then_inc(s_down, 1)

            run_slots(pe, slot, 4, NTF, NTF)


def decoder_layer(nc, a, out, stages=3):
    x1 = nc.dram_tensor("x1", [NT, P, 2, E], F32, kind="Internal").ap()
    x2 = nc.dram_tensor("x2", [NT, P, 2, E], F32, kind="Internal").ap()
    cs = nc.dram_tensor("cos_sin", [2, P, NSEQ * SEQ], F32, kind="Internal").ap()
    scratch = nc.dram_tensor("split_parts", [2, 2, E // NG, NG // EC, 2, EC * TOK], F16, kind="Internal").ap()
    scratch_x = nc.dram_tensor("split_parts_x", [2, 2, E // NG, NG // EC, 2, EC * TOK], F16, kind="Internal").ap()

    def chunks(w):
        return w.rearrange("(k p) n -> p k n", p=P)

    rotary_tables(nc, a["pos"], a["rot_cols"], cs)
    attention(nc, 16, 16, False,
              {"tok": a["x_tok"].rearrange("(t r p) e -> t p r e", r=2, p=P), "T": chunks(a["x_T"])}, None,
              {n: chunks(a["s_" + n]) for n in ("wq", "wk", "wv", "wo")},
              x1 if stages > 1 else out.rearrange("(t r p) e -> t p r e", r=2, p=P),
              {"scratch": scratch, **{n: a[n] for n in ("ident", "mask_q", "mask_k", "q_rows", "head_rows")},
               "bo": a["s_bo"], "bv": a["s_bv"], "bqk": a["s_bqk"], "k_rows": a["s_k_rows"]})
    if stages < 2:
        return
    attention(nc, 32, 8, True, {"tok": x1}, chunks(a["ctx_T"]),
              {n: chunks(a["x_" + n]) for n in ("wq", "wk", "wv", "wo")},
              x2 if stages > 2 else out.rearrange("(t r p) e -> t p r e", r=2, p=P),
              {"scratch": scratch_x, "ident": a["ident"], "head_rows": a["x_head_rows"], "bo": a["x_bo"], "k_rows": a["x_k_rows"],
               "cs": cs.rearrange("a p n -> p a n")})
    if stages < 3:
        return
    ffn(nc, x2.rearrange("(t a) p r e -> t p a r e", a=2),
        {"wg": chunks(a["wg"]), "wu": chunks(a["wu"]), "wd": chunks(a["wd"])},
        out.rearrange("(t r p) e -> t p r e", r=4, p=P), {"ident": a["ident"]})


def layout(inputs):
    import numpy as np

    g = {k: np.asarray(v) for k, v in inputs.items()}
    copy = np.ascontiguousarray

    def rows(b):
        return copy(np.broadcast_to(b, (P, b.shape[0])))

    def out_weights(w, d):
        return copy(w.reshape(E // d // 2, 2, d, E).transpose(1, 0, 2, 3).reshape(E, E))

    def split16(v):
        hi = v.astype(np.float16)
        return hi, (v - hi.astype(np.float64)).astype(np.float16)

    def grouped(w, d):
        lead = w.shape[:-1]
        return copy(np.moveaxis(w.reshape(*lead, NG // EC, EC, E // NG), -2, -3).reshape(*lead, E))

    def head_rows(d):
        rows_of = np.arange(3 * E // NG) % (E // NG) // d
        return copy((rows_of[:, None] == np.arange(E // NG // d)).astype(np.float32))

    x = g["x"].reshape(-1, E)
    pos = g["fside_BxSx2_0"].reshape(-1, 2)
    channel = np.arange(P) % 8
    a = {
        "x_tok": copy(x), "x_T": copy(x.T),
        "ctx_T": copy(g["ctx_1024"].reshape(-1, CTX).T),
        "pos": copy(pos.T[channel // 4]),
        "s_wq": grouped(g["L0_attn_Wq"].T, 16), "s_wk": grouped(g["L0_attn_Wk"].T, 16), "s_wv": copy(g["L0_attn_Wv"].T),
        "s_wo": out_weights(copy(g["L0_attn_Wo"].T), 16),
        "s_bqk": copy(np.stack([grouped(g[n], 16).reshape(EC, P).T for n in ("L0_attn_bq", "L0_attn_bk")], 1)),
        "s_bv": rows(g["L0_attn_bv"]), "s_bo": rows(g["L0_attn_bo"]),
        "x_wq": grouped(g["L0_xattn_Wq"], 8), "x_wk": grouped(g["L0_xattn_Wkv"][:, :E], 8), "x_wv": copy(g["L0_xattn_Wkv"][:, E:]),
        "x_wo": out_weights(g["L0_xattn_Wout"], 8), "x_bo": rows(g["L0_xattn_bout"]),
        "wg": copy(g["L0_ffn_w_gate"].T), "wu": copy(g["L0_ffn_w_up"].T), "wd": copy(g["L0_ffn_w_down"].T),
    }
    freqs = (np.float32(10000.0) ** (-np.arange(2, dtype=np.float32) / np.float32(2))).astype(np.float32)
    a["rot_cols"] = np.stack([freqs[channel % 4 // 2], np.where(channel % 2, 1.0, -1.0)], 1).astype(np.float32)
    a["ident"] = np.eye(P, dtype=np.float32)
    i = np.arange(P)[:, None] % SEQ
    j = np.arange(512)[None] % SEQ
    a["mask_q"] = np.where(j > i, -1e30, 0.0).astype(np.float32)
    a["mask_k"] = np.where(i > j, -1e30, 0.0).astype(np.float32)
    start = 2.0 ** -0.5
    slopes = np.array([start * start ** h for h in range(16)], np.float32).astype(np.float64)
    at = np.arange(TOK) % SEQ
    hi, lo = split16(slopes.reshape(NG, 2, 1) * at)
    one = np.ones((NG, TOK), np.float16)
    a["s_k_rows"] = copy(np.stack([hi[:, 0], lo[:, 0], hi[:, 1], lo[:, 1], one, one, -one]))
    q_rows = np.zeros((SELF_CONST, NG, BPT, 2, SEQ), np.float16)
    q_rows[0:2, :, :, 0] = 1
    q_rows[2:4, :, :, 1] = 1
    q_rows[4] = -hi[:, :, :SEQ][:, None]
    q_rows[5] = -lo[:, :, :SEQ][:, None]
    a["q_rows"] = q_rows.reshape(SELF_CONST, NG, BPT, 2 * SEQ)
    a["x_k_rows"] = copy(-one[None])
    a["head_rows"], a["x_head_rows"] = head_rows(16), head_rows(8)
    return a


def kernel(**inputs):
    import numpy as np
    from concourse import bacc
    from concourse.bass_utils import run_bass_kernel_spmd

    nc = bacc.Bacc("TRN2", target_bir_lowering=False, num_devices=1)
    arrays = layout(inputs)
    args = {n: nc.dram_tensor(f"in_{n}", v.shape, mybir.dt.from_np(v.dtype), kind="ExternalInput").ap()
            for n, v in arrays.items()}
    out = nc.dram_tensor("out", [NSEQ * SEQ, E], F32, kind="ExternalOutput").ap()
    decoder_layer(nc, args, out)
    got = run_bass_kernel_spmd(nc, [{f"in_{n}": v for n, v in arrays.items()}], core_ids=[0]).results[0]["out"]
    return np.asarray(got).reshape(NSEQ, SEQ, E)
```

```python
from contextlib import ExitStack

import concourse.bass as bass
from concourse import mybir

F32 = mybir.dt.float32
F32R = mybir.dt.float32r
F16 = mybir.dt.float16
BF16 = mybir.dt.bfloat16
ALU = mybir.AluOpType
ACT = mybir.ActivationFunctionType
AX_X = mybir.AxisListType.X

P = 128
SEQ = 64
NSEQ = 64
E = 256
CTX = 128
HID = 1024
TOK = 256
NT = NSEQ * SEQ // TOK
BPT = TOK // SEQ
NG = 8
EC = E // P
VW = 64
LN_EPS = 1e-5
M_CLAMP = 60000.0
SELF_CONST = 6
TWO_PI = (6.28125, 0.0019350051879882812, 3.0199159819149963e-07)
INV_TWO_PI = 0.15915494309189535
ROUND = 12582912.0
PI_IN = 3.1415925
HALF_PI = 1.5707963267948966


class Tile:

    def __init__(self, turn, parity):
        self.turn, self.parity = turn, parity
        self.n = turn * 2 + parity

    def back(self, k):
        m = self.parity - k
        return Tile(self.turn + m // 2 if m >= 0 else self.turn - (-m + 1) // 2, m % 2)


def there(t, tiles=NT):
    return not isinstance(t.n, int) or 0 <= t.n < tiles


def nth(t, per_tile, k):
    return t.n * per_tile + k


def dmas(t, count):
    return (t.turn + 1) * (16 * count)


def is_slot(s, n):
    return isinstance(s.n, int) and s.n == n


def waits_alone(eng):
    eng.nop(nofuse=True)


def run_slots(eng, slot, loop_from, last, tiles=NT, first=0):
    def peeled(slots):
        for s in slots:
            slot(Tile(s // 2, s % 2))

    peeled(range(first, loop_from))
    with eng.Fori(loop_from // 2, tiles // 2 - 1) as turn:
        for parity in range(2):
            slot(Tile(turn, parity))
    peeled(range(tiles - 2, last + 1))


def mm3(nc, out, w_hi, w_lo, x_hi, x_lo, first, last):
    nc.tensor.matmul(out, w_hi, x_hi, start=first, stop=False)
    nc.tensor.matmul(out, w_hi, x_lo, start=False, stop=False)
    return nc.tensor.matmul(out, w_lo, x_hi, start=False, stop=last)


class Weights:

    def __init__(self, nc, ctx, name, dram, scale):
        self.nc, self.name, self.dram, self.scale = nc, name, dram, scale
        self.raw, self.hi, self.lo, self.loaded = {}, {}, {}, {}
        for n, w in dram.items():
            self.hi[n], self.lo[n] = (ctx.enter_context(nc.sbuf_tensor(f"{name}_{n}_{part}", list(w.shape), F32R))
                                      for part in ("hi", "lo"))
            self.loaded[n] = ctx.enter_context(nc.semaphore(f"{name}_{n}_loaded"))
        self.hi_done = ctx.enter_context(nc.semaphore(f"{name}_high"))
        self.lo_done = ctx.enter_context(nc.semaphore(f"{name}_low"))
        self.pieces = [(n, slice(k, k + step)) for n, w in dram.items()
                       for step in (min(w.shape[1], max(1, 1024 // w.shape[2])),)
                       for k in range(0, w.shape[1], step)]

    def __getitem__(self, n):
        return self.hi[n], self.lo[n]

    def stage(self, ctx):
        for n, w in self.dram.items():
            self.raw[n] = ctx.enter_context(self.nc.sbuf_tensor(f"{self.name}_{n}_raw", list(w.shape), F32))

    def load(self, eng):
        for n, w in self.dram.items():
            eng.dma_start(self.raw[n][:], w).then_inc(self.loaded[n], 16)

    def share(self, k, of):
        return range(k * len(self.pieces) // of, (k + 1) * len(self.pieces) // of)

    def split_high(self, act, p):
        n, k = self.pieces[p]
        act.wait_ge(self.loaded[n], 16)
        self.nc.scalar.activation(self.hi[n][:, k], self.raw[n][:, k], ACT.Copy,
                                  scale=self.scale.get(n, 1.0)).then_inc(self.hi_done, 1)

    def split_low(self, eng, unit, p):
        n, k = self.pieces[p]
        eng.wait_ge(self.hi_done, p + 1)
        lo, raw, hi = self.lo[n][:, k], self.raw[n][:, k], self.hi[n][:, k].bitcast(F32)
        if n in self.scale:
            unit.scalar_tensor_tensor(lo, raw, self.scale[n], hi, ALU.mult, ALU.subtract).then_inc(self.lo_done, 1)
        else:
            unit.tensor_tensor(lo, raw, hi, ALU.subtract).then_inc(self.lo_done, 1)


class RotaryTables:
    ROWS = 4 * NT

    def __init__(self, nc, ctx, pos_dram, freq_dram, table):
        def sb(name, shape):
            return ctx.enter_context(nc.sbuf_tensor(f"r_{name}", shape, F32))

        self.nc, self.pos_dram, self.freq_dram = nc, pos_dram, freq_dram
        self.by_channel = table.rearrange("(a r) t k n -> r k a t n", r=2)
        self.pos, self.turns, self.cos, self.minus_sin = (
            sb(n, [self.ROWS, TOK]) for n in ("pos", "turns", "cos", "minus_sin"))
        self.freq = sb("freq", [self.ROWS, 1])
        self.loaded, self.step, self.sined, self.stored = (
            ctx.enter_context(nc.semaphore(f"r_{n}")) for n in ("loaded", "step", "sined", "stored"))

    def load(self, sp):
        sp.dma_start(self.pos[:], self.pos_dram).then_inc(self.loaded, 16)
        sp.dma_start(self.freq[:], self.freq_dram).then_inc(self.loaded, 16)

    def angles(self, dve):
        nc, pos, turns, cos, step = self.nc, self.pos, self.turns, self.cos, self.step
        dve.wait_ge(self.loaded, 32)
        nc.vector.tensor_scalar(pos[:], pos[:], self.freq[:, 0:1], None, ALU.mult).then_inc(step, 1)
        dve.wait_ge(step, 1)
        nc.vector.tensor_scalar(turns[:], pos[:], INV_TWO_PI, ROUND, ALU.mult, ALU.add).then_inc(step, 1)
        dve.wait_ge(step, 2)
        nc.vector.tensor_scalar(turns[:], turns[:], ROUND, None, ALU.subtract).then_inc(step, 1)
        for k, part in enumerate(TWO_PI):
            dve.wait_ge(step, 3 + k)
            nc.vector.scalar_tensor_tensor(pos[:], turns[:], -part, pos[:], ALU.mult, ALU.add).then_inc(step, 1)
        dve.wait_ge(step, 6)
        nc.vector.tensor_scalar(pos[:], pos[:], PI_IN, -PI_IN, ALU.min, ALU.max).then_inc(step, 1)
        dve.wait_ge(step, 7)
        nc.vector.scalar_tensor_tensor(cos[:], pos[:], -1.0, pos[:], ALU.mult, ALU.max).then_inc(step, 1)
        dve.wait_ge(step, 8)
        nc.vector.tensor_scalar(cos[:], cos[:], -1.0, HALF_PI, ALU.mult, ALU.add).then_inc(step, 1)

    def sines(self, act):
        act.wait_ge(self.step, 9)
        self.nc.scalar.activation(self.pos[:], self.pos[:], ACT.Sin).then_inc(self.sined, 1)
        self.nc.scalar.activation(self.cos[:], self.cos[:], ACT.Sin).then_inc(self.sined, 1)

    def negative(self, dve):
        dve.wait_ge(self.sined, 2)
        self.nc.vector.tensor_scalar(self.minus_sin[:], self.pos[:], -1.0, None, ALU.mult).then_inc(self.step, 1)

    def store(self, sp):
        sp.wait_ge(self.step, 10)
        for r, k, value in ((0, 0, self.cos), (1, 0, self.cos), (0, 1, self.minus_sin), (1, 1, self.pos)):
            sp.dma_start(self.by_channel[r, k], value[:]).then_inc(self.stored, 16)

    def wait_stored(self, sp):
        sp.wait_ge(self.stored, 64)


def attention(nc, heads, d_head, rope, src, kv_src, weights, x_out, stored, consts, ident, tables=None, ahead=(),
              src_stored=None, next_loads=()):
    G = heads // NG
    SPLIT = 3 * d_head * G
    CONST = 0 if rope else SELF_CONST
    ROWS_M = SPLIT + CONST
    ROWS_X = ROWS_M + 1
    NX = heads * SEQ // 512
    MCOL = NG * BPT * G // 2
    VS = 2 * (d_head + 1)
    OW = 28 if rope else VW
    KC = 1 if rope else EC
    pre = "x" if rope else "s"

    with ExitStack() as ctx:
        def sb(name, shape, dt):
            return ctx.enter_context(nc.sbuf_tensor(f"{pre}_{name}", shape, dt))

        def ps(name, shape):
            return ctx.enter_context(nc.psum_tensor(f"{pre}_{name}", shape, F32))

        def sem(name):
            return ctx.enter_context(nc.semaphore(f"{pre}_{name}"))

        wq, wk, wv, wo = (weights[n] for n in ("wq", "wk", "wv", "wo"))
        qin = None if rope else [sb(f"qin{i}", [P, EC, TOK], F32) for i in range(2)]
        kvin = [sb(f"kvin{i}", [P, KC, TOK], F32) for i in range(2)] if rope else None
        tok_a = [sb(f"toka{i}", [P, 2, E], F32) for i in range(2)] if rope else None
        tok_in = [sb(f"tok{i}", [P, 2, E], F32) for i in range(2)]
        kv_hi = [sb(f"kv_hi{i}", [P, KC, TOK], F32R) for i in range(2)]
        kv_lo = [sb(f"kv_lo{i}", [P, KC, TOK], F32R) for i in range(2)]
        q_hi = [sb("q_hi", [P, EC, TOK], F32R)] if rope else kv_hi
        q_lo = [sb("q_lo", [P, EC, TOK], F32R)] if rope else kv_lo
        qk16 = sb("qk16", [P, 2, 2, EC, TOK], F16)
        if rope:
            cs = [sb(f"cs{i}", [P, 2, TOK], F32) for i in range(2)]
            rot = sb("rot", [P, 2, 3, EC, TOK], F32)
        K3 = [sb(f"K3{i}", [ROWS_X, NG, TOK], F16) for i in range(2)]
        Qr = sb("Qr", [SPLIT, NG, TOK], F16)
        head_rows = sb("head_rows", [SPLIT, G], F32)
        Q3 = [sb(f"Q3{i}", [ROWS_X, NG, BPT, G * SEQ], F16) for i in range(2)]
        Vb = [sb(f"Vb{i}", [P, 2, heads * VS + VW], F32) for i in range(2)]
        PT = [sb(f"PT{i}", [P, heads * SEQ], F32) for i in range(2)]
        mx = sb("mx", [P, MCOL], F32)
        mT = sb("mT", [MCOL, P], F16)
        rec = sb("rec", [P, 2, heads // 2, 2], F32)
        On = sb("On", [P, 2, 2, E // 2], F32)
        aT_hi, aT_lo = sb("aT_hi", [P, 2, 2, P], F32R), sb("aT_lo", [P, 2, 2, P], F32R)
        y = sb("y", [P, 2, E], F32)
        stats = sb("stats", [P, 2, 6], F32)
        mv = sb("mv", [P, 2, 2], F32)
        rstd = sb("rstd", [P, 2], F32)
        shift = sb("shift", [P, 2], F32)
        x_new = [sb(f"xn{i}", [P, 2, E], F32) for i in range(2)]
        bo_bc = sb("bo", [P, E], F32)
        minus_half = sb("mh", [P, 1], F32)
        if not rope:
            ident_bf = sb("identb", [P, P], BF16)
            mask_q = sb("mask_q", [P, 512], BF16)
            mask_k = sb("mask_k", [P, 512], BF16)
            mask_raw = PT[0][:].rearrange("p (m n) -> p m n", m=2)
            bv_bc = sb("bv", [P, E], F32)
            bqk = sb("bqk", [P, 2, EC], F32)

        psX = [ps(f"psX{i}", [P, 512]) for i in range(2)]
        psM = [ps(f"psM{i}", [P, 512]) for i in range(2)]
        psJ = [ps(f"psJ{i}", [P, 512]) for i in range(2)]
        psO = ps("psO", [P, 2, 512])

        s_first = sem("first_const_loaded")
        s_const = sem("const_loaded")
        s_in = [sem(f"in_loaded{i}") for i in range(2)]
        s_cs = [sem(f"cos_sin_loaded{i}") for i in range(2)]
        s_tok = [sem(f"tok_loaded{i}") for i in range(2)]
        s_init = sem("buffers_set")
        s_bq = sem("bq_scaled")
        s_mask = sem("masks_cast")
        s_split = sem("inputs_split")
        s_qkproj = sem("qk_projected")
        s_hi = sem("qk_high")
        s_lo = sem("qk_low")
        s_vproj = sem("v_projected")
        s_vb = sem("v_placed")
        s_scr = [sem(f"{n}_parts_stored") for n in "qk"]
        s_qr = sem("q_rows_loaded")
        s_k3 = [sem(f"k_rows_loaded{i}") for i in range(2)]
        s_q3 = [sem(f"q_spread_{n}") for n in ("act", "dve")]
        s_mscore = sem("max_scores")
        s_mx = sem("maxima")
        s_mtr = sem("maxima_transposed")
        s_mt = sem("maxima_copied")
        s_mrow = [sem(f"shift_rows{i}") for i in range(2)]
        s_xscore = sem("scores")
        s_exp = sem("probs")
        s_pv = sem("pv_done")
        s_rec = sem("sums_inverted")
        s_on = sem("normalised")
        s_atr = sem("attn_transposed")
        s_ahi = sem("attn_high")
        s_alo = sem("attn_low")
        s_proj = sem("out_projected")
        s_xb = sem("residual_biased")
        s_y = sem("residual_added")
        s_stat = sem("stats_done")
        s_var = sem("variance_done")
        s_eps = sem("eps_added")
        s_rstd = sem("rstd_done")
        s_shift = sem("norm_shift_done")
        s_new = sem("normed")
        s_store = stored
        if rope:
            s_xtr = sem("input_transposed")
            s_xhi = sem("input_high")
            s_xlo = sem("input_low")
            s_plain = sem("rot_plain")
            s_swap = sem("rot_swapped")
            s_cos = sem("rot_by_cos")
            s_sin = [sem(f"{n}_by_sin") for n in "qk"]
            s_rot = sem("rotated")
        scratch = consts["scratch"]
        n_in = 2 if rope else 1
        hi_per = 2 if rope else 4
        STEPS = 2 * NX
        i_chunk = [slice(SEQ * b, SEQ * (b + 1)) for b in range(BPT)]

        first_loads = [] if rope else [(bqk[:], consts["bqk"]), (ident[:], consts["ident"])]
        const_loads = [(head_rows[:], consts["head_rows"])]
        if not rope:
            const_loads += [(mask_raw[:, 0], consts["mask_q"]), (mask_raw[:, 1], consts["mask_k"]),
                            (bv_bc[:], consts["bv"])]
        const_loads += [(bo_bc[:], consts["bo"])]
        for i in range(2):
            const_loads += [(K3[i][SPLIT:ROWS_X, :, :], consts["k_rows"])]
            if not rope:
                const_loads += [(Q3[i][SPLIT:ROWS_M], consts["q_rows"])]
        def aT_ps():
            return psJ[0][:, 0:2 * P].rearrange("p (b r q) -> p b r q", b=2, r=2)

        def po(pr):
            return psO[:, pr, 0:OW * heads // 2].rearrange("p (h w) -> p h w", w=OW)[:, :, 0:2 * (d_head + 1)].rearrange(
                "p h (b e) -> p h b e", e=d_head + 1)

        def cs_of(n):
            return consts["cs"][n].rearrange("(o c) m -> o c m", o=1).to_broadcast([P // 8, 8, 2 * TOK])

        def ahead_pieces(s):
            k = s.n - (NT - 2) if isinstance(s.n, int) and not rope else -1
            return ahead[1].share(k, 3) if 0 <= k < 3 else ()

        def v_of(i, rows, b):
            return Vb[i][rows, :, 0:heads * VS].rearrange("p r (h w) -> p r h w", w=VS)[
                :, :, :, b * (d_head + 1):(b + 1) * (d_head + 1)]

        def by_sin(eng, unit, s, o):
            eng.wait_ge(s_swap, nth(s, 2, o + 1))
            eng.wait_ge(s_cs[s.parity], dmas(s, 1))
            unit.tensor_tensor(rot[:, o, 1], rot[:, o, 1], cs[s.parity][:, 1:2, :].to_broadcast([P, EC, TOK]),
                               ALU.mult).then_inc(s_sin[o], 1)

        spreads = range(1), range(1, G)

        def spread_q(eng, compute, s, who, part):
            i = s.parity
            eng.wait_ge(s_qr, nth(s, 48, 48))
            if there(s.back(2)):
                eng.wait_ge(s_xscore, nth(s.back(2), STEPS, STEPS))
            for h in spreads[who][part]:
                compute(Q3[i][0:SPLIT, :, :, bass.ts(h, SEQ)].rearrange("r g b q -> r (g b) q"),
                        Qr[:].rearrange("r g (b q) -> r (g b) q", q=SEQ), head_rows[:, h:h + 1])\
                    .then_inc(s_q3[who], 1)

        def wait_spread(eng, s):
            for done, heads_of in zip(s_q3, spreads):
                eng.wait_ge(done, nth(s, len(heads_of), len(heads_of)))
                waits_alone(eng)

        block = ctx.enter_context(nc.Block())

        @block.sync
        def _(sp):
            def slot(s):
                e, f, c, d = s.back(-1), s.back(-2), s.back(2), s.back(3)
                i = s.parity
                if rope and is_slot(s, 0):
                    for done in src_stored:
                        sp.wait_ge(done, 16 * NT // 2)
                if there(f):
                    if there(s):
                        sp.wait_ge(s_split, nth(s, 2, 2))
                        if rope:
                            waits_alone(sp)
                            sp.wait_ge(s_xtr, nth(s, 1, 1))
                        waits_alone(sp)
                    if rope:
                        sp.dma_start(tok_a[i][:], src["tok"][f.n]).then_inc(s_in[i], 16)
                        sp.dma_start(kvin[i][:], kv_src[:, :, bass.ds(f.n * TOK, TOK)]).then_inc(s_in[i], 16)
                    else:
                        sp.dma_start(qin[i][:], src["T"][:, :, bass.ds(f.n * TOK, TOK)]).then_inc(s_in[i], 16)
                if rope and there(e):
                    if there(s.back(1)):
                        sp.wait_ge(s_cos, nth(s.back(1), 2, 2))
                        waits_alone(sp)
                        for o in range(2):
                            sp.wait_ge(s_sin[o], nth(s.back(1), 1, 1))
                            waits_alone(sp)
                    sp.dma_start(cs[1 - i][:], cs_of(e.n)).then_inc(s_cs[1 - i], 16)
                if is_slot(s, -2):
                    if not rope:
                        weights.load(sp)
                    for dst, dram in first_loads:
                        sp.dma_start(dst, dram).then_inc(s_first, 16)
                if there(c):
                    if there(c.back(2)):
                        sp.wait_ge(s_y, nth(c.back(2), 2, 2))
                        waits_alone(sp)
                    sp.dma_start(tok_in[i][:], src["tok"][c.n]).then_inc(s_tok[i], 16)
                if there(s):
                    if there(c):
                        sp.wait_ge(s_k3[i], dmas(c, 3))
                        waits_alone(sp)
                    for o in range(2):
                        sp.wait_ge(s_hi, nth(s, hi_per, hi_per // 2 * (o + 1)))
                        sp.wait_ge(s_lo, nth(s, hi_per, hi_per // 2 * (o + 1)))
                        sp.dma_start(scratch[i, o].rearrange("r g a n -> g r (a n)"),
                                     qk16[:, o].rearrange("p a c n -> p (a c n)")).then_inc(s_scr[o], 16)
                        sp.wait_ge(s_scr[o], (s.n + 1) * 16)
                        waits_alone(sp)
                        if there(c):
                            if o:
                                sp.wait_ge(s_xscore, nth(c, STEPS, STEPS))
                            else:
                                wait_spread(sp, s.back(1))
                        for k, part in enumerate(((0, 1, 0), (0, 0, 1))[o]):
                            to = (Qr, K3[i])[o][bass.ts(k, E // NG)].rearrange("r g n -> r (g n)")
                            sp.dma_start(to, scratch[i, o, :, :, part]).then_inc((s_qr, s_k3[i])[o], 16)
                if not rope and is_slot(s, 0):
                    tables.load(sp)
                if not rope and is_slot(s, 1):
                    tables.store(sp)
                if not rope and is_slot(s, 2):
                    for w in ahead:
                        w.load(sp)
                if there(d):
                    sp.wait_ge(s_new, nth(d, 2, 2))
                    waits_alone(sp)
                    sp.dma_start(x_out[d.n], x_new[1 - i][:]).then_inc(s_store[1 - i], 16)

            run_slots(sp, slot, 4, NT + 2, first=-2)
            if not rope:
                tables.wait_stored(sp)

        @block.gpsimd
        def _(pool):
            nc.gpsimd.memset(minus_half[:], -0.5).then_inc(s_init, 1)
            for i in range(2):
                nc.gpsimd.memset(Vb[i][:], 0.0).then_inc(s_init, 1)
            pool.wait_ge(s_init, 3)
            for i in range(2):
                for b in range(2):
                    nc.gpsimd.memset(v_of(i, slice(b * SEQ, (b + 1) * SEQ), b)[:, :, :, d_head:d_head + 1],
                                     1.0).then_inc(s_init, 1)
                    pool.wait_ge(s_init, 4 + 2 * i + b)
            if not rope:
                pool.wait_ge(s_first, 16 * len(first_loads))
                nc.gpsimd.tensor_scalar(bqk[:, 0], bqk[:, 0], d_head ** -0.5, None, ALU.mult).then_inc(s_bq, 1)

            def by_cos(s, o):
                pool.wait_ge(s_plain, nth(s, 2, o + 1))
                if o == 0:
                    pool.wait_ge(s_cs[s.parity], dmas(s, 1))
                if there(s.back(1)):
                    pool.wait_ge(s_rot, nth(s.back(1), 2, o + 1))
                nc.gpsimd.tensor_tensor(rot[:, o, 2], rot[:, o, 0],
                                        cs[s.parity][:, 0:1, :].to_broadcast([P, EC, TOK]), ALU.mult).then_inc(s_cos, 1)

            def low_parts(s, o):
                pool.wait_ge(s_rot, nth(s, 2, o + 1))
                pool.wait_ge(s_hi, nth(s, 2, o + 1))
                if there(s.back(1)):
                    pool.wait_ge(s_scr[o], s.n * 16)
                nc.gpsimd.tensor_tensor(qk16[:, o, 1], rot[:, o, 1], qk16[:, o, 0], ALU.subtract).then_inc(s_lo, 1)

            def split_input(s):
                i = s.parity
                pool.wait_ge(s_in[i], dmas(s, n_in))
                if there(s.back(2)):
                    pool.wait_ge(s_vproj, nth(s.back(2), 1, 1))
                waits_alone(pool)
                raw = kvin[i] if rope else qin[i]
                nc.gpsimd.tensor_copy(kv_hi[i][:], raw[:]).then_inc(s_split, 1)
                pool.wait_ge(s_split, nth(s, 2, 1))
                nc.gpsimd.tensor_tensor(kv_lo[i][:], raw[:], kv_hi[i][:].bitcast(F32), ALU.subtract).then_inc(s_split, 1)

            def add_out_bias(c):
                i = c.parity
                pool.wait_ge(s_tok[i], dmas(c, 1))
                nc.gpsimd.tensor_tensor(tok_in[i][:], tok_in[i][:],
                                        bo_bc[:].rearrange("p (o n) -> p o n", o=1).to_broadcast([P, 2, E]),
                                        ALU.add).then_inc(s_xb, 1)

            def norm_factors(c, pr):
                pool.wait_ge(s_var, nth(c, 2, pr + 1))
                waits_alone(pool)
                nc.gpsimd.tensor_scalar(rstd[:, pr:pr + 1], mv[:, pr, 1:2], LN_EPS, None, ALU.add).then_inc(s_eps, 1)
                pool.wait_ge(s_eps, nth(c, 2, pr + 1))
                nc.gpsimd.tensor_tensor(rstd[:, pr:pr + 1], rstd[:, pr:pr + 1], minus_half[:],
                                        ALU.pow).then_inc(s_rstd, 1)
                pool.wait_ge(s_rstd, nth(c, 2, pr + 1))
                waits_alone(pool)
                nc.gpsimd.tensor_scalar(shift[:, pr:pr + 1], mv[:, pr, 0:1], rstd[:, pr:pr + 1], -1.0,
                                        ALU.mult, ALU.mult).then_inc(s_shift, 1)

            def slot(s):
                e, c, d = s.back(-1), s.back(2), s.back(3)
                if rope and there(s):
                    by_cos(s, 0)
                    by_cos(s, 1)
                    low_parts(s, 0)
                    by_sin(pool, nc.gpsimd, s, 1)
                    low_parts(s, 1)
                if there(d):
                    norm_factors(d, 1)
                if there(c):
                    add_out_bias(c)
                if there(e):
                    split_input(e)
                if is_slot(s, -1 if rope else 0):
                    for dst, dram in const_loads:
                        pool.dma_start(dst, dram).then_inc(s_const, 16)
                if is_slot(s, 0):
                    pool.wait_ge(s_const, 16 * len(const_loads))
                if there(c):
                    norm_factors(c, 0)
                for p in ahead_pieces(s):
                    ahead[1].split_low(pool, nc.gpsimd, p)

            run_slots(pool, slot, 6, NT + 2, first=-1)

        @block.scalar
        def _(act):
            if not rope:
                for p in range(len(weights.pieces)):
                    weights.split_high(act, p)
            if not rope:
                act.wait_ge(s_bq, 1)

            def high_parts(s, o):
                if there(s.back(1)):
                    act.wait_ge(s_scr[o], (s.n) * 16)
                if rope:
                    act.wait_ge(s_rot, nth(s, 2, o + 1))
                    nc.scalar.activation(qk16[:, o, 0], rot[:, o, 1], ACT.Copy).then_inc(s_hi, 1)
                    return
                act.wait_ge(s_qkproj, nth(s, 2, o + 1))
                for ch in range(EC):
                    nc.scalar.activation(qk16[:, o, 0, ch], psJ[o][:, bass.ts(ch, TOK)], ACT.Identity,
                                         bias=bqk[:, o, ch:ch + 1]).then_inc(s_hi, 1)

            def plain(s, o):
                act.wait_ge(s_qkproj, nth(s, 2, o + 1))
                if there(s.back(1)):
                    act.wait_ge(s_swap, nth(s.back(1), 2, o + 1))
                    act.wait_ge(s_cos, nth(s.back(1), 2, o + 1))
                nc.scalar.activation(rot[:, o, 0], psJ[o][:].rearrange("p (c n) -> p c n", c=EC), ACT.Copy,
                                     scale=1.0 if o else d_head ** -0.5).then_inc(s_plain, 1)

            def probs(c, k):
                pr, x = divmod(k, NX)
                act.wait_ge(s_xscore, nth(c, STEPS, k + 1))
                if there(c.back(1)):
                    act.wait_ge(s_pv, nth(c.back(1), 2, pr + 1))
                nc.scalar.activation(PT[pr][:, bass.ts(x, 512)], psX[k % 2][:], ACT.Exp).then_inc(s_exp, 1)

            def attn_high(c, pr):
                act.wait_ge(s_atr, nth(c, 2, pr + 1))
                if there(c.back(1)):
                    act.wait_ge(s_proj, nth(c.back(1), 2, pr + 1))
                nc.scalar.activation(aT_hi[:, pr].rearrange("p r (b q) -> p b r q", b=2), aT_ps(),
                                     ACT.Copy).then_inc(s_ahi, 1)

            def normed(c, pr):
                act.wait_ge(s_shift, nth(c, 2, pr + 1))
                if pr == 0 and there(c.back(2)):
                    act.wait_ge(s_store[c.parity], dmas(c.back(2), 1))
                nc.scalar.activation(x_new[c.parity][:, pr], y[:, pr], ACT.Identity, bias=shift[:, pr:pr + 1],
                                     scale=rstd[:, pr:pr + 1]).then_inc(s_new, 1)

            def by_rows(out, rows, factor):
                return nc.scalar.activation(out, rows, ACT.Copy, scale=factor)

            def input_high(e):
                act.wait_ge(s_xtr, nth(e, 1, 1))
                if there(e.back(1)):
                    act.wait_ge(s_qkproj, nth(e.back(1), 2, 1))
                nc.scalar.activation(q_hi[0][:], psJ[1][:].rearrange("p (c n) -> p c n", c=EC),
                                     ACT.Copy).then_inc(s_xhi, 1)

            def place_v(s):
                act.wait_ge(s_vproj, nth(s, 1, 1))
                for b in range(2):
                    rows = slice(b * SEQ, (b + 1) * SEQ)
                    nc.scalar.activation(v_of(s.parity, rows, b)[:, :, :, 0:d_head],
                                         psJ[1][rows, :].rearrange("p (r h e) -> p r h e", r=2, e=d_head),
                                         ACT.Copy).then_inc(s_vb, 1)

            def slot(s):
                e, b_, c, d = s.back(-1), s.back(1), s.back(2), s.back(3)
                if there(s):
                    for o in range(2):
                        plain(s, o) if rope else high_parts(s, o)
                for k in range(NX):
                    if there(c):
                        probs(c, k)
                    if k == 1 and there(s) and rope:
                        high_parts(s, 0)
                    if k == NX - 2 and there(d):
                        attn_high(d, 1)
                if there(d):
                    normed(d, 0)
                if rope and there(s):
                    high_parts(s, 1)
                for k in range(NX, STEPS):
                    if there(c):
                        probs(c, k)
                    if k == NX:
                        if rope and there(b_):
                            place_v(b_)
                    if there(c) and k == NX + NX // 2 - 1:
                        attn_high(c, 0)
                    if k == STEPS - 3 and rope and there(e):
                        input_high(e)
                    if k == STEPS - 2 and there(d):
                        normed(d, 1)
                if there(b_):
                    act.wait_ge(s_mt, nth(b_, 1, 1))
                    act.dma_start(Q3[b_.parity][ROWS_M:ROWS_X], mT[:]).then_inc(s_mrow[b_.parity], 16)
                if is_slot(s, NT):
                    for done in stored if next_loads else ():
                        act.wait_ge(done, 16 * 2)
                    for dst, dram, loaded in next_loads:
                        act.dma_start(dst, dram).then_inc(loaded, 16)
                if there(s):
                    if is_slot(s, 0):
                        act.wait_ge(s_const, 16 * len(const_loads))
                        act.wait_ge(s_init, 7)
                    spread_q(act, by_rows, s, 0, slice(None))
                if not rope and is_slot(s, 1):
                    tables.sines(act)
                for p in ahead_pieces(s):
                    ahead[1].split_high(act, p)
                if not rope and is_slot(s, NT - 1):
                    for p in range(len(ahead[0].pieces)):
                        ahead[0].split_high(act, p)

            run_slots(act, slot, 4, NT + 2, first=-1)

        @block.vector
        def _(dve):
            if not rope:
                for p in range(len(weights.pieces)):
                    weights.split_low(dve, nc.vector, p)
            def set_constants():
                dve.wait_ge(s_const, 16 * len(const_loads))
                dve.wait_ge(s_init, 7)
                if not rope:
                    nc.vector.tensor_copy(mask_q[:], mask_raw[:, 0]).then_inc(s_mask, 1)
                    nc.vector.tensor_copy(mask_k[:], mask_raw[:, 1]).then_inc(s_mask, 1)
                    nc.vector.tensor_copy(ident_bf[:], ident[:]).then_inc(s_mask, 1)

            def by_rows(out, rows, factor):
                return nc.vector.tensor_scalar(out, rows, factor, None, ALU.mult)

            def low_parts(s, o):
                dve.wait_ge(s_hi, nth(s, 4, 2 * o + 2))
                for ch in range(EC):
                    nc.vector.scalar_tensor_tensor(qk16[:, o, 1, ch], psJ[o][:, bass.ts(ch, TOK)],
                                                   bqk[:, o, ch:ch + 1], qk16[:, o, 0, ch],
                                                   ALU.add, ALU.subtract).then_inc(s_lo, 1)

            def swapped(s, o):
                dve.wait_ge(s_plain, nth(s, 2, o + 1))
                if there(s.back(1)):
                    dve.wait_ge(s_lo, nth(s.back(1), 2, o + 1))
                    dve.wait_ge(s_hi, nth(s.back(1), 2, o + 1))
                waits_alone(dve)
                nc.vector.stream_shuffle(rot[:, o, 1], rot[:, o, 0], [n ^ 1 for n in range(32)]).then_inc(s_swap, 1)

            def rotated(s, o):
                dve.wait_ge(s_sin[o], nth(s, 1, 1))
                dve.wait_ge(s_cos, nth(s, 2, o + 1))
                nc.vector.tensor_tensor(rot[:, o, 1], rot[:, o, 1], rot[:, o, 2], ALU.add).then_inc(s_rot, 1)

            def maxima(b_, m):
                dve.wait_ge(s_mscore, nth(b_, STEPS, m + 1))
                if m == 0 and there(b_.back(1)):
                    dve.wait_ge(s_mtr, nth(b_.back(1), 1, 1))
                nc.vector.tensor_reduce(mx[:, bass.ts(m, 8)], psM[m % 2][:].rearrange("p (c k) -> p c k", k=SEQ),
                                        AX_X, ALU.max).then_inc(s_mx, 1)

            def normalise(c, pr):
                dve.wait_ge(s_pv, nth(c, 2, pr + 1))
                o = po(pr)
                nc.vector.reciprocal(rec[:, pr], o[:, :, :, d_head:d_head + 1].rearrange("p h b e -> p h (b e)"))\
                    .then_inc(s_rec, 1)
                dve.wait_ge(s_rec, nth(c, 2, pr + 1))
                if there(c.back(1)):
                    dve.wait_ge(s_atr, nth(c.back(1), 2, pr + 1))
                nc.vector.tensor_tensor(
                    On[:, pr].rearrange("p b (h e) -> p b h e", e=d_head),
                    o[:, :, :, 0:d_head].rearrange("p h b e -> p b h e"),
                    rec[:, pr].rearrange("p h (b e) -> p b h e", e=1).to_broadcast([P, 2, heads // 2, d_head]),
                    ALU.mult).then_inc(s_on, 1)

            def attn_low(c, pr):
                dve.wait_ge(s_ahi, nth(c, 2, pr + 1))
                nc.vector.tensor_tensor(aT_lo[:, pr].rearrange("p r (b q) -> p b r q", b=2), aT_ps(),
                                        aT_hi[:, pr].bitcast(F32).rearrange("p r (b q) -> p b r q", b=2),
                                        ALU.subtract).then_inc(s_alo, 1)

            def place_v(s):
                dve.wait_ge(s_vproj, nth(s, 1, 1))
                for b in range(2):
                    rows = slice(b * SEQ, (b + 1) * SEQ)
                    out = v_of(s.parity, rows, b)[:, :, :, 0:d_head]
                    v = psJ[1][rows, :].rearrange("p (r h e) -> p r h e", r=2, e=d_head)
                    bias = bv_bc[rows, :].rearrange("p (r h e) -> p r h e", r=1, e=d_head)
                    nc.vector.tensor_tensor(out, v, bias.to_broadcast([SEQ, 2, heads, d_head]),
                                            ALU.add).then_inc(s_vb, 1)

            def residual(c, pr):
                dve.wait_ge(s_proj, nth(c, 2, pr + 1))
                dve.wait_ge(s_xb, nth(c, 1, 1))
                if there(c.back(1)):
                    dve.wait_ge(s_new, nth(c.back(1), 2, pr + 1))
                nc.vector.tensor_tensor(y[:, pr], psJ[0][:, 0:E], tok_in[c.parity][:, pr], ALU.add).then_inc(s_y, 1)
                dve.wait_ge(s_y, nth(c, 2, pr + 1))
                nc.vector.bn_stats(stats[:, pr], y[:, pr]).then_inc(s_stat, 1)
                dve.wait_ge(s_stat, nth(c, 2, pr + 1))
                waits_alone(dve)
                nc.vector.bn_aggr(mv[:, pr], stats[:, pr]).then_inc(s_var, 1)

            def input_low(e):
                dve.wait_ge(s_xhi, nth(e, 1, 1))
                nc.vector.tensor_tensor(q_lo[0][:], psJ[1][:].rearrange("p (c n) -> p c n", c=EC),
                                        q_hi[0][:].bitcast(F32), ALU.subtract).then_inc(s_xlo, 1)

            def shifts(b_):
                dve.wait_ge(s_mtr, nth(b_, 1, 1))
                if there(b_.back(1)):
                    dve.wait_ge(s_mrow[1 - b_.parity], dmas(b_.back(1), 1))
                nc.vector.tensor_scalar(mT[:], psJ[1][0:MCOL, 0:P], M_CLAMP, -M_CLAMP,
                                        ALU.min, ALU.max).then_inc(s_mt, 1)

            def slot(s):
                e, b_, c, d = s.back(-1), s.back(1), s.back(2), s.back(3)
                if there(s):
                    if rope:
                        swapped(s, 0)
                        by_sin(dve, nc.vector, s, 0)
                    else:
                        low_parts(s, 0)
                        low_parts(s, 1)
                for k in range(NX):
                    if k == 1 and there(s) and rope:
                        rotated(s, 0)
                    if k == NX - 1 and there(d):
                        attn_low(d, 1)
                    if there(b_):
                        maxima(b_, k)
                    if k == 1 and there(s) and rope:
                        swapped(s, 1)
                if rope and there(s):
                    rotated(s, 1)
                if there(d):
                    residual(d, 1)
                if there(c):
                    normalise(c, 0)
                if not rope and there(b_):
                    place_v(b_)
                for k in range(NX, STEPS):
                    if there(b_):
                        maxima(b_, k)
                    if k == STEPS - 2 and rope and there(e):
                        input_low(e)
                    if k == NX + NX // 2 - 1 and there(c):
                        attn_low(c, 0)
                if there(b_):
                    shifts(b_)
                if is_slot(s, 0):
                    set_constants()
                if there(s):
                    spread_q(dve, by_rows, s, 1, slice(0, 1))
                if there(c):
                    residual(c, 0)
                if there(s) and rope:
                    spread_q(dve, by_rows, s, 1, slice(1, None))
                if there(c):
                    normalise(c, 1)
                if not rope and is_slot(s, 1):
                    tables.angles(dve)
                    tables.negative(dve)
                if not rope and is_slot(s, NT):
                    for p in range(len(ahead[0].pieces)):
                        ahead[0].split_low(dve, nc.vector, p)

            run_slots(dve, slot, 4, NT + 2, first=-1)

        @block.tensor
        def _(pe):
            if not rope:
                pe.wait_ge(s_first, 16 * len(first_loads))


            def qk_copied(s, o):
                if rope:
                    pe.wait_ge(s_plain, nth(s, 2, o + 1))
                else:
                    pe.wait_ge(s_lo, nth(s, 4, 2 * o + 2))

            def project(s, o):
                if is_slot(s, 0):
                    pe.wait_ge(weights.lo_done, o + 1)
                w, hi, lo = (wk, kv_hi, kv_lo) if o else (wq, q_hi, q_lo)
                x_hi, x_lo = (hi[s.parity], lo[s.parity]) if o or not rope else (hi[0], lo[0])
                n_k = KC if o else EC
                for ch in range(EC):
                    for k in range(n_k):
                        last = mm3(nc, psJ[o][:, bass.ts(ch, TOK)], w[0][:, k, bass.ts(ch, P)],
                                   w[1][:, k, bass.ts(ch, P)], x_hi[:, k], x_lo[:, k], k == 0, k == n_k - 1)
                last.then_inc(s_qkproj, 1)

            def max_scores(b_, m):
                if m or there(b_.back(1)):
                    if not (m == 1 and not there(b_.back(1))):
                        pe.wait_ge(s_mx, nth(b_, STEPS, m - 1))
                if m == 0:
                    wait_spread(pe, b_)
                    pe.wait_ge(s_k3[b_.parity], dmas(b_, 3))
                out, i = psM[m % 2], b_.parity
                if not rope:
                    nc.tensor.matmul(out[:], ident_bf[:], mask_q[:], start=True, stop=True, skip_group_check=True)
                for k in range(8):
                    g, b, a = (m * 8 + k) // (BPT * G // 2), (m * 8 + k) // (G // 2) % BPT, k % (G // 2)
                    last = nc.tensor.matmul(out[:, bass.ts(k, SEQ)], Q3[i][0:ROWS_M, g, b, bass.ts(a, P)],
                                            K3[i][0:ROWS_M, g, i_chunk[b]], start=rope and k == 0, stop=True,
                                            skip_group_check=True)
                last.then_inc(s_mscore, 1)

            def scores(c, k):
                pr, x = divmod(k, NX)
                i, out = c.parity, psX[k % 2]
                if k > 1 or there(c.back(1)):
                    pe.wait_ge(s_exp, nth(c, STEPS, k - 1))
                if k == 0:
                    pe.wait_ge(s_mrow[i], dmas(c, 1))
                if not rope:
                    nc.tensor.matmul(out[:], ident_bf[:], mask_k[:], start=True, stop=True, skip_group_check=True)
                n_g = 8 // G
                for b in range(2):
                    for n in range(n_g):
                        g, b4 = x * n_g + n, 2 * pr + b
                        last = nc.tensor.matmul(out[b * SEQ:(b + 1) * SEQ, bass.ts(n, G * SEQ)],
                                                K3[i][0:ROWS_X, g, i_chunk[b4]], Q3[i][0:ROWS_X, g, b4],
                                                start=rope and n == 0, stop=True, skip_group_check=True)
                last.then_inc(s_xscore, 1)

            def attend(c, k):
                pr, x = divmod(k, NX)
                if x == 0:
                    pe.wait_ge(s_vb, nth(c, 2, 2))
                    if there(c.back(1)):
                        pe.wait_ge(s_on, nth(c.back(1), 2, pr + 1))
                pe.wait_ge(s_exp, nth(c, STEPS, k + 1))
                for h in range(8 * x, 8 * x + 8):
                    col = h // 2 * OW
                    last = nc.tensor.matmul(psO[(h % 2) * SEQ:(h % 2 + 1) * SEQ, pr, col:col + VW],
                                            PT[pr][:, bass.ts(h, SEQ)], Vb[c.parity][:, pr, h * VS:h * VS + VW],
                                            start=True, stop=True, skip_group_check=True)
                if x == NX - 1:
                    last.then_inc(s_pv, 1)

            def transpose_attn(c, pr):
                pe.wait_ge(s_on, nth(c, 2, pr + 1))
                for b in range(2):
                    last = nc.tensor.transpose(psJ[0][:, bass.ts(b, P)], On[:, pr, b], ident[:])
                last.then_inc(s_atr, 1)

            def project_out(c, pr):
                pe.wait_ge(s_alo, nth(c, 2, pr + 1))
                for r in range(2):
                    last = mm3(nc, psJ[0][:, 0:E], aT_hi[:, pr, r], aT_lo[:, pr, r], wo[0][:, r], wo[1][:, r],
                               r == 0, r == 1)
                last.then_inc(s_proj, 1)

            def transpose_input(e):
                pe.wait_ge(s_in[e.parity], dmas(e, n_in))
                if there(e.back(2)):
                    pe.wait_ge(s_vb, nth(e.back(2), 2, 2))
                elif there(e.back(1)):
                    qk_copied(e.back(1), 1)
                for r in range(2):
                    for ch in range(EC):
                        last = nc.tensor.transpose(psJ[1][:, ch * TOK + r * P:ch * TOK + (r + 1) * P],
                                                   tok_a[e.parity][:, r, bass.ts(ch, P)], ident[:])
                last.then_inc(s_xtr, 1)

            def project_v(s):
                for pr in range(2):
                    for k in range(KC):
                        x = bass.ts(pr, P)
                        last = mm3(nc, psJ[1][:, bass.ts(pr, E)], kv_hi[s.parity][:, k, x], kv_lo[s.parity][:, k, x],
                                   wv[0][:, k], wv[1][:, k], k == 0, k == KC - 1)
                last.then_inc(s_vproj, 1)

            def transpose_maxima(b_):
                pe.wait_ge(s_mx, nth(b_, STEPS, STEPS))
                waits_alone(pe)
                nc.tensor.transpose(psJ[1][0:MCOL, 0:P], mx[:], ident[:]).then_inc(s_mtr, 1)

            def slot(s):
                e, b_, c, d = s.back(-1), s.back(1), s.back(2), s.back(3)
                if there(s):
                    if rope:
                        pe.wait_ge(s_xlo, nth(s, 1, 1))
                    else:
                        pe.wait_ge(s_split, nth(s, 2, 2))
                    if there(d):
                        pe.wait_ge(s_y, nth(d, 2, 1))
                    elif there(b_):
                        qk_copied(b_, 0)
                    project(s, 0)
                    if rope:
                        pe.wait_ge(s_split, nth(s, 2, 2))
                    if there(c):
                        pe.wait_ge(s_mt, nth(c, 1, 1))
                    elif there(b_):
                        qk_copied(b_, 1)
                    project(s, 1)
                if is_slot(s, 1):
                    pe.wait_ge(s_const, 16 * len(const_loads))
                    pe.wait_ge(s_init, 7)
                    pe.wait_ge(weights.lo_done, len(weights.pieces))
                    if not rope:
                        pe.wait_ge(s_mask, 3)
                for k in range(NX):
                    if k == NX - 1 and there(d):
                        if there(s):
                            qk_copied(s, 0)
                        else:
                            pe.wait_ge(s_y, nth(d, 2, 1))
                        transpose_attn(d, 1)
                    if there(c):
                        scores(c, k)
                    if there(b_):
                        max_scores(b_, k)
                    if there(c) and k:
                        attend(c, k - 1)
                if there(d):
                    project_out(d, 1)
                if there(c):
                    attend(c, NX - 1)
                if there(b_):
                    if there(s):
                        qk_copied(s, 1)
                    elif there(c):
                        pe.wait_ge(s_mt, nth(c, 1, 1))
                    project_v(b_)
                for k in range(NX, STEPS):
                    if k == NX + NX // 2 and there(c):
                        if there(d):
                            pe.wait_ge(s_y, nth(d, 2, 2))
                        elif there(s):
                            qk_copied(s, 0)
                        transpose_attn(c, 0)
                    if k == STEPS - 2 and rope and there(e):
                        transpose_input(e)
                    if there(c):
                        scores(c, k)
                    if there(b_):
                        max_scores(b_, k)
                    if there(c) and k > NX:
                        attend(c, k - 1)
                if there(b_):
                    if rope and there(e):
                        pe.wait_ge(s_xlo, nth(e, 1, 1))
                    else:
                        pe.wait_ge(s_vb, nth(b_, 2, 2))
                    transpose_maxima(b_)
                if there(c):
                    project_out(c, 0)
                    attend(c, STEPS - 1)

            run_slots(pe, slot, 4, NT + 2, first=-1)


def ffn(nc, x_in, x_stored, inputs, weights, out, ident):
    FT = 4
    N = FT * P
    NTF = NSEQ * SEQ // N
    HC = HID // P

    with ExitStack() as ctx:
        def sb(name, shape, dt):
            return ctx.enter_context(nc.sbuf_tensor(f"f_{name}", shape, dt))

        def ps(name, shape):
            return ctx.enter_context(nc.psum_tensor(f"f_{name}", shape, F32))

        def sem(name):
            return ctx.enter_context(nc.semaphore(f"f_{name}"))

        wg, wu, wd = (weights[n] for n in ("wg", "wu", "wd"))
        x_tok, s_in = inputs
        x_res = [sb(f"x_res{i}", [P, FT, E], F32) for i in range(2)]
        x_hi = [sb(f"x_hi{i}", [P, EC, N], F32R) for i in range(2)]
        x_lo = [sb(f"x_lo{i}", [P, EC, N], F32R) for i in range(2)]
        gate = [sb(f"gate{i}", [P, N], F32) for i in range(2)]
        hid = [sb(f"hid{i}", [P, N], F32) for i in range(2)]
        h_hi = [sb(f"h_hi{i}", [P, HC, N], F32R) for i in range(2)]
        h_lo = [sb(f"h_lo{i}", [P, HC, N], F32R) for i in range(2)]
        y = sb("y", [P, FT, E], F32)
        stats = sb("stats", [P, FT, 6], F32)
        mv = sb("mv", [P, FT, 2], F32)
        rstd = sb("rstd", [P, FT], F32)
        x_new = [sb(f"xn{i}", [P, FT, E], F32) for i in range(2)]
        minus_half = sb("mh", [P, FT], F32)

        psT = [ps(f"psT{i}", [P, N]) for i in range(2)]
        psG = [ps(f"psG{i}", [P, N]) for i in range(2)]
        psU = [ps(f"psU{i}", [P, N]) for i in range(2)]
        psD = [ps(f"psD{i}", [P, 2, E]) for i in range(2)]

        s_init = sem("constants_set")
        s_res = [sem(f"res_loaded{i}") for i in range(2)]
        s_xtr = sem("input_transposed")
        s_xhi = sem("input_high")
        s_xlo = sem("input_low")
        s_gate = sem("gate_done")
        s_up = sem("up_done")
        s_silu = sem("silu_done")
        s_h = sem("hidden_done")
        s_hhi = sem("hidden_high")
        s_hlo = sem("hidden_low")
        s_down = sem("down_done")
        s_y = sem("residual_added")
        s_stat = sem("stats_done")
        s_var = sem("variance_done")
        s_eps = sem("eps_added")
        s_rstd = sem("rstd_done")
        s_new = sem("normed")
        s_store = [sem(f"out_stored{i}") for i in range(2)]
        block = ctx.enter_context(nc.Block())

        def is_tile(t):
            return there(t, NTF)

        @block.sync
        def _(sp):
            def slot(s):
                e, f, c, i = s.back(-1), s.back(-2), s.back(1), s.parity
                if is_slot(s, 0):
                    for done in x_stored:
                        sp.wait_ge(done, 16 * NT // 2)
                if is_tile(f) and is_tile(s):
                    sp.wait_ge(s_xtr, nth(s, 1, 1))
                    waits_alone(sp)
                    sp.dma_start(x_tok[i][:].rearrange("p (a r) e -> p a r e", a=2), x_in[f.n])\
                        .then_inc(s_in[i], 16)
                if is_tile(s):
                    if is_tile(s.back(2)):
                        sp.wait_ge(s_y, nth(s.back(2), 2, 2))
                        waits_alone(sp)
                    sp.dma_start(x_res[i][:].rearrange("p (a r) e -> p a r e", a=2), x_in[s.n])\
                        .then_inc(s_res[i], 16)
                if is_tile(c):
                    for half in range(2):
                        rows = slice(2 * half, 2 * half + 2)
                        sp.wait_ge(s_new, nth(c, FT, 2 * half + 2))
                        waits_alone(sp)
                        sp.dma_start(out[c.n][:, rows], x_new[1 - i][:, rows]).then_inc(s_store[1 - i], 16)

            run_slots(sp, slot, 2, NTF, NTF, first=-2)
            for i in range(2):
                sp.wait_ge(s_store[i], 32 * NTF // 2)

        @block.scalar
        def _(act):
            def input_high(e):
                for ch in range(EC):
                    act.wait_ge(s_xtr, nth(e, 1, 1))
                    if is_tile(e.back(2)):
                        act.wait_ge(s_up, nth(e.back(2), HC, HC))
                    nc.scalar.activation(x_hi[e.parity][:, ch], psT[ch][:], ACT.Copy).then_inc(s_xhi, 1)

            def slot(s):
                e = s.back(-1)
                if not is_tile(s):
                    if is_tile(e):
                        input_high(e)
                    return
                for h in range(HC):
                    b = h % 2
                    act.wait_ge(s_gate, nth(s, HC, h + 1))
                    if h > 1 or is_tile(s.back(1)):
                        act.wait_ge(s_h, nth(s, HC, h - 1))
                    nc.scalar.activation(gate[b][:], psG[b][:], ACT.Silu).then_inc(s_silu, 1)
                    act.wait_ge(s_h, nth(s, HC, h + 1))
                    if is_tile(s.back(2)):
                        act.wait_ge(s_down, nth(s.back(2), FT, FT))
                    nc.scalar.activation(h_hi[s.parity][:, h], hid[b][:], ACT.Copy).then_inc(s_hhi, 1)
                    if h == HC - 3 and is_tile(e):
                        input_high(e)

            run_slots(act, slot, 2, NTF - 1, NTF, first=-1)

        @block.vector
        def _(dve):
            def input_low(e):
                for ch in range(EC):
                    dve.wait_ge(s_xhi, nth(e, EC, ch + 1))
                    nc.vector.tensor_tensor(x_lo[e.parity][:, ch], psT[ch][:], x_hi[e.parity][:, ch].bitcast(F32),
                                            ALU.subtract).then_inc(s_xlo, 1)

            def slot(s):
                e, c = s.back(-1), s.back(1)
                if is_slot(s, -1):
                    input_low(e)
                for h in range(HC):
                    b = h % 2
                    if is_tile(s):
                        dve.wait_ge(s_silu, nth(s, HC, h + 1))
                        dve.wait_ge(s_up, nth(s, HC, h + 1))
                        if h > 1 or is_tile(s.back(1)):
                            dve.wait_ge(s_hlo, nth(s, HC, h - 1))
                        nc.vector.tensor_tensor(hid[b][:], gate[b][:], psU[b][:], ALU.mult).then_inc(s_h, 1)
                        if h == HC - 3 and is_tile(e):
                            input_low(e)
                    if is_tile(c) and h in (4, 7):
                        half = h // 7
                        dve.wait_ge(s_down, nth(c, FT, 2 * half + 2))
                        dve.wait_ge(s_res[c.parity], dmas(c, 1))
                        if is_tile(c.back(1)):
                            dve.wait_ge(s_new, nth(c.back(1), FT, 2 * half + 2))
                        nc.vector.tensor_tensor(y[:, 2 * half:2 * half + 2], psD[half][:],
                                                x_res[c.parity][:, 2 * half:2 * half + 2], ALU.add).then_inc(s_y, 1)
                        dve.wait_ge(s_y, nth(c, 2, half + 1))
                        for r in range(2 * half, 2 * half + 2):
                            nc.vector.bn_stats(stats[:, r], y[:, r]).then_inc(s_stat, 1)
                        dve.wait_ge(s_stat, nth(c, FT, 2 * half + 2))
                        waits_alone(dve)
                        for r in range(2 * half, 2 * half + 2):
                            nc.vector.bn_aggr(mv[:, r], stats[:, r]).then_inc(s_var, 1)

            run_slots(dve, slot, 2, NTF, NTF, first=-1)

        @block.gpsimd
        def _(pool):
            nc.gpsimd.memset(minus_half[:], -0.5).then_inc(s_init, 1)
            pool.wait_ge(s_init, 1)

            def slot(s):
                c = s.back(1)
                for h in range(HC):
                    if is_tile(s):
                        pool.wait_ge(s_hhi, nth(s, HC, h + 1))
                        nc.gpsimd.tensor_tensor(h_lo[s.parity][:, h], hid[h % 2][:],
                                                h_hi[s.parity][:, h].bitcast(F32), ALU.subtract).then_inc(s_hlo, 1)
                    if is_tile(c) and h in (5, 7):
                        half = h // 7
                        rows = slice(2 * half, 2 * half + 2)
                        pool.wait_ge(s_var, nth(c, FT, 2 * half + 2))
                        waits_alone(pool)
                        nc.gpsimd.tensor_scalar(rstd[:, rows], mv[:, rows, 1:2].rearrange("p r e -> p (r e)"), LN_EPS,
                                                None, ALU.add).then_inc(s_eps, 1)
                        pool.wait_ge(s_eps, nth(c, 2, half + 1))
                        nc.gpsimd.tensor_tensor(rstd[:, rows], rstd[:, rows], minus_half[:, rows],
                                                ALU.pow).then_inc(s_rstd, 1)
                        pool.wait_ge(s_rstd, nth(c, 2, half + 1))
                        if half == 0 and is_tile(c.back(2)):
                            pool.wait_ge(s_store[c.parity], dmas(c.back(2), 2))
                        waits_alone(pool)
                        for r in range(2 * half, 2 * half + 2):
                            nc.gpsimd.tensor_scalar(x_new[c.parity][:, r], y[:, r], mv[:, r, 0:1], rstd[:, r:r + 1],
                                                    ALU.subtract, ALU.mult).then_inc(s_new, 1)

            run_slots(pool, slot, 4, NTF, NTF)

        @block.tensor
        def _(pe):
            pe.wait_ge(weights.lo_done, len(weights.pieces))

            def transpose_input(e):
                pe.wait_ge(s_in[e.parity], dmas(e, 1))
                if is_tile(e.back(1)):
                    pe.wait_ge(s_xlo, nth(e.back(1), EC, EC))
                for ch in range(EC):
                    for r in range(FT):
                        last = nc.tensor.transpose(psT[ch][:, bass.ts(r, P)], x_tok[e.parity][:, r, bass.ts(ch, P)],
                                                   ident[:])
                last.then_inc(s_xtr, 1)

            def slot(s):
                e, c = s.back(-1), s.back(1)
                if is_slot(s, -1):
                    transpose_input(e)
                if is_tile(s):
                    pe.wait_ge(s_xlo, nth(s, EC, EC))
                for h in range(HC):
                    if is_tile(s):
                        if h > 1 or is_tile(c):
                            pe.wait_ge(s_silu, nth(s, HC, h - 1))
                            pe.wait_ge(s_h, nth(s, HC, h - 1))
                        for w, bank, done in ((wg, psG[h % 2], s_gate), (wu, psU[h % 2], s_up)):
                            for k in range(EC):
                                last = mm3(nc, bank[:], w[0][:, k, bass.ts(h, P)], w[1][:, k, bass.ts(h, P)],
                                           x_hi[s.parity][:, k], x_lo[s.parity][:, k], k == 0, k == EC - 1)
                            last.then_inc(done, 1)
                        if h == HC - 4 and is_tile(e):
                            transpose_input(e)
                    if is_tile(c) and h % 2:
                        r = h // 2
                        if r == 0:
                            pe.wait_ge(s_hlo, nth(c, HC, HC))
                        if is_tile(c.back(1)):
                            pe.wait_ge(s_y, nth(c.back(1), 2, r // 2 + 1))
                        for k in range(HC):
                            x = bass.ts(r, P)
                            last = mm3(nc, psD[r // 2][:, r % 2], h_hi[c.parity][:, k, x], h_lo[c.parity][:, k, x],
                                       wd[0][:, k], wd[1][:, k], k == 0, k == HC - 1)
                        last.then_inc(s_down, 1)

            run_slots(pe, slot, 2, NTF, NTF, first=-1)


def decoder_layer(nc, a, out):
    x1 = nc.dram_tensor("x1", [NT, P, 2, E], F32, kind="Internal").ap()
    x2 = nc.dram_tensor("x2", [NT, P, 2, E], F32, kind="Internal").ap()
    table = nc.dram_tensor("cos_sin", [8, NT, 2, TOK], F32, kind="Internal").ap()
    scratch = nc.dram_tensor("split_parts", [2, 2, E // NG, NG // EC, 2, EC * TOK], F16, kind="Internal").ap()
    scratch_x = nc.dram_tensor("split_parts_x", [2, 2, E // NG, NG // EC, 2, EC * TOK], F16, kind="Internal").ap()

    def chunks(w):
        return w.rearrange("(k p) n -> p k n", p=P)

    def weights(ctx, pre, names, scale={}):
        return Weights(nc, ctx, pre, {n: chunks(a[pre + n]) for n in names}, scale)

    attn_w = ("wq", "wk", "wv", "wo")
    with ExitStack() as ctx:
        ffn_w = weights(ctx, "f_", ("wg", "wu", "wd"))
        cross_w = weights(ctx, "x_", attn_w)
        ident = ctx.enter_context(nc.sbuf_tensor("ident", [P, P], F32))
        x2_ffn = x2.rearrange("(t a) p r e -> t p a r e", a=2)
        f_in = [ctx.enter_context(nc.semaphore(f"f_in_loaded{i}")) for i in range(2)]
        x1_stored, x2_stored = ([ctx.enter_context(nc.semaphore(f"{n}_stored{i}")) for i in range(2)]
                                for n in ("x1", "x2"))
        with ExitStack() as self_ctx:
            self_w = weights(self_ctx, "s_", attn_w, {"wq": 16 ** -0.5})
            for w in (ffn_w, cross_w, self_w):
                w.stage(self_ctx)
            tables = RotaryTables(nc, self_ctx, a["pos"], a["freq"], table)
            attention(nc, 16, 16, False,
                      {"tok": a["x_tok"].rearrange("(t r p) e -> t p r e", r=2, p=P), "T": chunks(a["x_T"])}, None,
                      self_w, x1, x1_stored,
                      {"scratch": scratch, **{n: a[n] for n in ("ident", "mask_q", "mask_k", "q_rows", "head_rows")},
                       "bo": a["s_bo"], "bv": a["s_bv"], "bqk": a["s_bqk"], "k_rows": a["s_k_rows"]},
                      ident, tables, [cross_w, ffn_w])
        x_tok = [ctx.enter_context(nc.sbuf_tensor(f"f_x_tok{i}", [P, 4, E], F32)) for i in range(2)]
        ffn_loads = [(x_tok[i][:].rearrange("p (a r) e -> p a r e", a=2), x2_ffn[i], f_in[i]) for i in range(2)]
        attention(nc, 32, 8, True, {"tok": x1}, chunks(a["ctx_T"]), cross_w, x2, x2_stored,
                  {"scratch": scratch_x, "head_rows": a["x_head_rows"], "bo": a["x_bo"],
                   "k_rows": a["x_k_rows"], "cs": table.rearrange("c t k n -> t c (k n)")}, ident,
                  src_stored=x1_stored, next_loads=ffn_loads)
        ffn(nc, x2_ffn, x2_stored, (x_tok, f_in), ffn_w,
            out.rearrange("(t r p) e -> t p r e", r=4, p=P), ident)


def layout(inputs):
    import numpy as np

    g = {k: np.asarray(v) for k, v in inputs.items()}
    copy = np.ascontiguousarray

    def rows(b):
        return copy(np.broadcast_to(b, (P, b.shape[0])))

    def out_weights(w, d):
        return copy(w.reshape(E // d // 2, 2, d, E).transpose(1, 0, 2, 3).reshape(E, E))

    def split16(v):
        hi = v.astype(np.float16)
        return hi, (v - hi.astype(np.float64)).astype(np.float16)

    def grouped(w, d):
        lead = w.shape[:-1]
        return copy(np.moveaxis(w.reshape(*lead, NG // EC, EC, E // NG), -2, -3).reshape(*lead, E))

    def head_rows(d):
        rows_of = np.arange(3 * E // NG) % (E // NG) // d
        return copy((rows_of[:, None] == np.arange(E // NG // d)).astype(np.float32))

    x = g["x"].reshape(-1, E)
    pos = g["fside_BxSx2_0"].reshape(-1, 2)
    angle = np.arange(4)
    a = {
        "x_tok": copy(x), "x_T": copy(x.T),
        "ctx_T": copy(g["ctx_1024"].reshape(-1, CTX).T),
        "pos": copy(pos.T.reshape(2, NT, TOK)[angle // 2].reshape(-1, TOK)),
        "s_wq": grouped(g["L0_attn_Wq"].T, 16), "s_wk": grouped(g["L0_attn_Wk"].T, 16), "s_wv": copy(g["L0_attn_Wv"].T),
        "s_wo": out_weights(copy(g["L0_attn_Wo"].T), 16),
        "s_bqk": copy(np.stack([grouped(g[n], 16).reshape(EC, P).T for n in ("L0_attn_bq", "L0_attn_bk")], 1)),
        "s_bv": rows(g["L0_attn_bv"]), "s_bo": rows(g["L0_attn_bo"]),
        "x_wq": grouped(g["L0_xattn_Wq"], 8), "x_wk": grouped(g["L0_xattn_Wkv"][:, :E], 8), "x_wv": copy(g["L0_xattn_Wkv"][:, E:]),
        "x_wo": out_weights(g["L0_xattn_Wout"], 8), "x_bo": rows(g["L0_xattn_bout"]),
        "f_wg": copy(g["L0_ffn_w_gate"].T), "f_wu": copy(g["L0_ffn_w_up"].T), "f_wd": copy(g["L0_ffn_w_down"].T),
    }
    freqs = (np.float32(10000.0) ** (-np.arange(2, dtype=np.float32) / np.float32(2))).astype(np.float32)
    a["freq"] = copy(np.repeat(freqs[angle % 2], NT)[:, None])
    a["ident"] = np.eye(P, dtype=np.float32)
    i = np.arange(P)[:, None] % SEQ
    j = np.arange(512)[None] % SEQ
    a["mask_q"] = np.where(j > i, -1e30, 0.0).astype(np.float32)
    a["mask_k"] = np.where(i > j, -1e30, 0.0).astype(np.float32)
    start = 2.0 ** -0.5
    slopes = np.array([start * start ** h for h in range(16)], np.float32).astype(np.float64)
    at = np.arange(TOK) % SEQ
    hi, lo = split16(slopes.reshape(NG, 2, 1) * at)
    one = np.ones((NG, TOK), np.float16)
    a["s_k_rows"] = copy(np.stack([hi[:, 0], lo[:, 0], hi[:, 1], lo[:, 1], one, one, -one]))
    q_rows = np.zeros((SELF_CONST, NG, BPT, 2, SEQ), np.float16)
    q_rows[0:2, :, :, 0] = 1
    q_rows[2:4, :, :, 1] = 1
    q_rows[4] = -hi[:, :, :SEQ][:, None]
    q_rows[5] = -lo[:, :, :SEQ][:, None]
    a["q_rows"] = q_rows.reshape(SELF_CONST, NG, BPT, 2 * SEQ)
    a["x_k_rows"] = copy(-one[None])
    a["head_rows"], a["x_head_rows"] = head_rows(16), head_rows(8)
    return a


def kernel(**inputs):
    import numpy as np
    from concourse import bacc
    from concourse.bass_utils import run_bass_kernel_spmd

    nc = bacc.Bacc("TRN2", target_bir_lowering=False, num_devices=1)
    arrays = layout(inputs)
    args = {n: nc.dram_tensor(f"in_{n}", v.shape, mybir.dt.from_np(v.dtype), kind="ExternalInput").ap()
            for n, v in arrays.items()}
    out = nc.dram_tensor("out", [NSEQ * SEQ, E], F32, kind="ExternalOutput").ap()
    decoder_layer(nc, args, out)
    got = run_bass_kernel_spmd(nc, [{f"in_{n}": v for n, v in arrays.items()}], core_ids=[0]).results[0]["out"]
    return np.asarray(got).reshape(NSEQ, SEQ, E)
```
